# Optimizing a Trainium2 kernel written in Bass

```python
import numpy as np
import jax
import jax.numpy as jnp

def _softmax(x, axis=-1):
    return jax.nn.softmax(x, axis=axis)

def _gelu(x):
    return jax.nn.gelu(x, approximate=True)

def _silu(x):
    return jax.nn.silu(x)

def _sigmoid(x):
    return jax.nn.sigmoid(x)

def _layernorm(x, axis=-1, eps=1e-05):
    m = jnp.mean(x, axis=axis, keepdims=True)
    v = jnp.var(x, axis=axis, keepdims=True)
    return (x - m) / jnp.sqrt(v + eps)

def _scatter_add(tgt, idx, src, axis=0):
    return tgt.at[idx].add(src)

def _segment_sum(src, seg, n):
    return jax.ops.segment_sum(src, seg, n)
kernel_name = 'mk_gnn_ffn_d1_gnn_r64_52285f'

def setup_inputs(seed: int=0):
    np.random.seed(seed)
    _w = jnp.asarray

    def _rec_inputs():
        import jax
        import jax.numpy as jnp
        _gk = jax.random.key(seed)
        x = -0.000125 + 0.9999 * jax.random.normal(jax.random.fold_in(_gk, 1), (1024, 512), jnp.float32)
        src = jax.random.randint(jax.random.fold_in(_gk, 2), (16384,), 0, 1024, jnp.int32)
        dst = jax.random.randint(jax.random.fold_in(_gk, 3), (16384,), 0, 1024, jnp.int32)
        _o = jnp.argsort(dst, stable=True)
        src = src[_o]
        dst = dst[_o]
        edge_weight = jax.random.uniform(jax.random.fold_in(_gk, 12), (16384,), jnp.float32, 0.0, 0.999998)
        return (x, src, dst, edge_weight)
    x, src, dst, edge_weight = _rec_inputs()

    def _L0_gnn_setup():
        import jax, jax.numpy as jnp
        import numpy as np
        N_NODES = 1024
        key = jax.random.key(seed)
        k1, k2, k3, k4, k5 = jax.random.split(key, 5)
        in_dim, out_dim, n_edges = (512, 512, 8192)
        H = jax.random.normal(k1, (N_NODES, in_dim), dtype=jnp.float32)
        stdv = 1.0 / np.sqrt(out_dim)
        W = jax.random.uniform(k2, (in_dim, out_dim), minval=-stdv, maxval=stdv, dtype=jnp.float32)
        bias = jnp.zeros((out_dim,), dtype=jnp.float32)
        edge_row = jax.random.randint(k3, (n_edges,), 0, N_NODES, dtype=jnp.int32)
        edge_col = jax.random.randint(k4, (n_edges,), 0, N_NODES, dtype=jnp.int32)
        edge_val = jax.random.uniform(k5, (n_edges,), dtype=jnp.float32)
        return {'H': H, 'W': W, 'bias': bias, 'edge_row': edge_row, 'edge_col': edge_col, 'edge_val': edge_val}
    _L0_gnn_all = _L0_gnn_setup()
    _L0_gnn_in = {k: v for k, v in _L0_gnn_all.items() if k in ('W', 'bias')}
    del _L0_gnn_all

    def _L0_ffn_setup():
        import jax, jax.numpy as jnp
        import numpy as np
        B, S, D = (1, 64, 512)
        E, K, H = (64, 2, 256)
        HS = 32
        EPS = 1e-05
        key = jax.random.key(seed)
        ks = jax.random.split(key, 16)
        n = lambda k, shp, s=0.02: jax.random.normal(k, shp, dtype=jnp.float32) * s
        return {'x': jax.random.normal(ks[0], (B, S, D), dtype=jnp.float32), 'Wg': n(ks[1], (E, D)), 'bg': n(ks[2], (E,)), 'gamma': 1.0 + n(ks[3], (E, D)), 'beta': n(ks[4], (E, D)), 'W1': n(ks[5], (E, D, H)), 'b1': n(ks[6], (E, H)), 'W3': n(ks[7], (E, D, H)), 'b3': n(ks[8], (E, H)), 'W2': n(ks[9], (E, H, D)), 'b2': n(ks[10], (E, D)), 'gs': 1.0 + n(ks[11], (D,)), 'bs': n(ks[11], (D,)), 'Ws1': n(ks[12], (D, HS)), 'bs1': n(ks[12], (HS,)), 'Ws3': n(ks[13], (D, HS)), 'bs3': n(ks[13], (HS,)), 'Ws2': n(ks[14], (HS, D)), 'bs2': n(ks[15], (D,))}
    _L0_ffn_all = _L0_ffn_setup()
    _L0_ffn_in = {k: v for k, v in _L0_ffn_all.items() if k in ('Wg', 'bg', 'gamma', 'beta', 'W1', 'b1', 'W3', 'b3', 'W2', 'b2', 'gs', 'bs', 'Ws1', 'bs1', 'Ws3', 'bs3', 'Ws2', 'bs2')}
    del _L0_ffn_all
    return {'x': x, 'src': src, 'dst': dst, 'edge_weight': edge_weight, 'L0_gnn_W': _L0_gnn_in['W'], 'L0_gnn_bias': _L0_gnn_in['bias'], 'L0_ffn_Wg': _L0_ffn_in['Wg'], 'L0_ffn_bg': _L0_ffn_in['bg'], 'L0_ffn_gamma': _L0_ffn_in['gamma'], 'L0_ffn_beta': _L0_ffn_in['beta'], 'L0_ffn_W1': _L0_ffn_in['W1'], 'L0_ffn_b1': _L0_ffn_in['b1'], 'L0_ffn_W3': _L0_ffn_in['W3'], 'L0_ffn_b3': _L0_ffn_in['b3'], 'L0_ffn_W2': _L0_ffn_in['W2'], 'L0_ffn_b2': _L0_ffn_in['b2'], 'L0_ffn_gs': _L0_ffn_in['gs'], 'L0_ffn_bs': _L0_ffn_in['bs'], 'L0_ffn_Ws1': _L0_ffn_in['Ws1'], 'L0_ffn_bs1': _L0_ffn_in['bs1'], 'L0_ffn_Ws3': _L0_ffn_in['Ws3'], 'L0_ffn_bs3': _L0_ffn_in['bs3'], 'L0_ffn_Ws2': _L0_ffn_in['Ws2'], 'L0_ffn_bs2': _L0_ffn_in['bs2']}

def reference(x, src, dst, edge_weight, L0_gnn_W, L0_gnn_bias, L0_ffn_Wg, L0_ffn_bg, L0_ffn_gamma, L0_ffn_beta, L0_ffn_W1, L0_ffn_b1, L0_ffn_W3, L0_ffn_b3, L0_ffn_W2, L0_ffn_b2, L0_ffn_gs, L0_ffn_bs, L0_ffn_Ws1, L0_ffn_bs1, L0_ffn_Ws3, L0_ffn_bs3, L0_ffn_Ws2, L0_ffn_bs2):
    import jax
    import jax.numpy as jnp

    def _L0_gnn_ref(H, W, bias, edge_row, edge_col, edge_val):
        import jax, jax.numpy as jnp
        import numpy as np
        N_NODES = 1024
        HW = H @ W
        msgs = edge_val[:, None] * HW[edge_col]
        out = jax.ops.segment_sum(msgs, edge_row, num_segments=N_NODES)
        out = out + bias
        return jax.nn.relu(out)

    def _L0_ffn_ref(x, Wg, bg, gamma, beta, W1, b1, W3, b3, W2, b2, gs, bs, Ws1, bs1, Ws3, bs3, Ws2, bs2):
        import jax, jax.numpy as jnp
        import numpy as np
        B, S, D = (1, 64, 512)
        E, K, H = (64, 2, 256)
        HS = 32
        EPS = 1e-05
        shape = x.shape
        xt = x.reshape(-1, D)
        T = xt.shape[0]
        scores = jax.nn.sigmoid(xt @ Wg.T + bg)
        w, idx = jax.lax.top_k(scores, K)
        w = w / w.sum(-1, keepdims=True)
        cw = jnp.zeros((T, E), xt.dtype).at[jnp.arange(T)[:, None], idx].add(w)
        mu = xt.mean(-1, keepdims=True)
        var = ((xt - mu) ** 2).mean(-1, keepdims=True)
        nx = (xt - mu) * jax.lax.rsqrt(var + EPS)
        W1p = gamma[:, :, None] * W1
        b1p = b1 + jnp.einsum('ed,edh->eh', beta, W1)
        W3p = gamma[:, :, None] * W3
        b3p = b3 + jnp.einsum('ed,edh->eh', beta, W3)
        h1 = jnp.einsum('td,edh->eth', nx, W1p) + b1p[:, None, :]
        h3 = jnp.einsum('td,edh->eth', nx, W3p) + b3p[:, None, :]
        h = jax.nn.silu(h1) * h3
        hw = h * cw.T[:, :, None]
        y = jnp.einsum('eth,ehd->td', hw, W2) + cw @ b2
        nxs = nx * gs + bs
        hs = jax.nn.silu(nxs @ Ws1 + bs1) * (nxs @ Ws3 + bs3)
        z = hs @ Ws2 + bs2
        return (y + z).reshape(shape)
    x = x + _L0_gnn_ref(_layernorm(x, axis=-1), L0_gnn_W, L0_gnn_bias, src, dst, edge_weight)
    x = x + _L0_ffn_ref(_layernorm(x, axis=-1)[None], L0_ffn_Wg, L0_ffn_bg, L0_ffn_gamma, L0_ffn_beta, L0_ffn_W1, L0_ffn_b1, L0_ffn_W3, L0_ffn_b3, L0_ffn_W2, L0_ffn_b2, L0_ffn_gs, L0_ffn_bs, L0_ffn_Ws1, L0_ffn_bs1, L0_ffn_Ws3, L0_ffn_bs3, L0_ffn_Ws2, L0_ffn_bs2)[0]
    return x

_drawn_inputs = setup_inputs


def setup_inputs(seed=0):
    import zlib

    import numpy as np

    out = dict(_drawn_inputs(seed))
    spreads = {'L0_gnn_bias': (0.0, 0.1)}
    factors = {'L0_ffn_Wg': 2.8,
     'L0_ffn_bg': 8.0,
     'L0_ffn_gamma': 8.0,
     'L0_ffn_beta': 8.0,
     'L0_ffn_W1': 3.243,
     'L0_ffn_b1': 8.0,
     'L0_ffn_W3': 3.181,
     'L0_ffn_b3': 8.0,
     'L0_ffn_W2': 3.184,
     'L0_ffn_b2': 5.57,
     'L0_ffn_gs': 8.0,
     'L0_ffn_bs': 8.0,
     'L0_ffn_Ws1': 6.345,
     'L0_ffn_bs1': 8.0,
     'L0_ffn_Ws3': 6.176,
     'L0_ffn_bs3': 8.0,
     'L0_ffn_Ws2': 6.207,
     'L0_ffn_bs2': 3.941}
    for name, (base, spread) in spreads.items():
        noise = np.random.default_rng([zlib.crc32(name.encode()), seed]).standard_normal(out[name].shape)
        drawn = base * np.exp(spread * noise) if base else spread * noise
        out[name] = jnp.asarray(drawn.astype(out[name].dtype))
    for name, factor in factors.items():
        out[name] = (out[name] * factor).astype(out[name].dtype)
    return out
```

```python
import numpy as np
import concourse.bass as bass
from concourse import mybir
from contextlib import ExitStack

N, D = 1024, 512
EDGES = 16384
EXPERTS, HID, HS = 64, 256, 32
EPS = 1e-5
P = 128
NB = N // P
DC = D // P
HC = HID // P
TILES = EDGES // P
WIN = 16
QUAD = 4
CAP = 80
ROUNDS = -(-N // CAP)
LIST = ROUNDS * CAP
REC = 4
RING = 8
GROUPS = EXPERTS // RING
NOWHERE = 60000.0


def moe_gnn(nc, x, src, dst, ew, W, bias, Wg, bg, gamma, beta, W1, b1, W3, b3, W2, b2,
            gs, bs, Ws1, bs1, Ws3, bs3, Ws2, bs2, out):
    f32, i32, u32 = mybir.dt.float32, mybir.dt.int32, mybir.dt.uint32
    ALU = mybir.AluOpType
    ACT = mybir.ActivationFunctionType
    AX = mybir.AxisListType.X
    ds = bass.ds

    ctx = ExitStack()
    with ctx:
        def sb(name, shape, dt=f32):
            return ctx.enter_context(nc.sbuf_tensor(name, shape, dt))

        def sem(name):
            return ctx.enter_context(nc.semaphore(name))

        nx_rows = nc.dram_tensor("nx_rows", (N, D), f32).ap()
        slots = nc.dram_tensor("slots", (EXPERTS * LIST, REC), f32).ap()
        y_rows = nc.dram_tensor("y_rows", (2 * N, D), f32).ap()

        w13 = sb("w13", [P, RING, 2, DC, HID])
        w2 = sb("w2", [P, RING, HC, D])
        X = sb("X", [P, NB, D])
        A = sb("A", [P, (N + WIN) * 8])
        HW = sb("HW", [P, NB, D])
        GW = sb("GW", [P, DC, D])
        osl = sb("osl", [P, 2, 8, P])
        M = sb("M", [P, 2, QUAD, P])
        xh = sb("xh", [P, 2, D])
        xhT = sb("xhT", [P, 2, DC, P])
        AT = sb("AT", [P, 2, NB, P])
        eT = sb("eT", [P, 3, P])
        wrow = sb("wrow", [1, 2 * P])
        wbase = wrow[:, P:2 * P].bitcast(i32)
        rounds_sb = sb("rounds_sb", [1, 2], i32)
        ident = sb("ident", [P, P])
        ones = sb("ones", [P, P])
        iota = sb("iota", [P, P])
        tokcol = sb("tokcol", [P, 1])
        eps_c = sb("eps_c", [P, 1])
        mhalf = sb("mhalf", [P, 1])
        stats = sb("stats", [P, 6 * NB])
        mv = sb("mv", [P, NB, 2])
        rstd = sb("rstd", [P, NB])
        gT = sb("gT", [P, DC, EXPERTS])
        bT = sb("bT", [P, DC, EXPERTS])
        b13T = sb("b13T", [P, 2, HC, EXPERTS])
        R = sb("R", [P, DC, P])
        bc = sb("bc", [P, P])
        rowWg = sb("rowWg", [P, EXPERTS])
        gs4 = sb("gs4", [P, 2, DC])
        small = sb("small", [P, 256])

        raw_wg, raw_g, raw_b = AT[0:64, 0, 0:4, :], AT[0:64, 0, 4:8, :], AT[0:64, 1, 0:4, :]
        raw_b13 = AT[0:64, 1, 4:8, :]
        edge_src, edge_dst = xhT[:, 0, 0, :].bitcast(i32), xhT[:, 0, 1, :].bitcast(i32)
        edge_w = xhT[:, 0, 2, :]
        d8 = xhT[:, 0, 3, :].bitcast(i32)
        shi = xhT[:, 1, 0, :].bitcast(i32)
        slo = xhT[:, 1, 1, :].bitcast(i32)
        key = xhT[:, 1, 2, :]
        slof = xhT[:, 1, 3, :]
        Ws = xh[:, 0, 0:4 * 64].rearrange("p (c n) -> p c n", c=DC)
        Wsb = xh[:, 0, 4 * 64:8 * 64].rearrange("p (c n) -> p c n", c=DC)
        sentinel = HW[:, 0:5, :].rearrange("p b d -> p (b d)")[:, 0:EXPERTS * LIST * REC // P]
        biasB = M[:, 0, :, :].rearrange("p a b -> p (a b)")
        stackB = M[0:97, 1, :, :].rearrange("p a b -> p (a b)")
        route_buf = osl[:, :, :, :].rearrange("p a b c -> p (a b c)")
        xt = route_buf[:, 0:512]
        nx = [route_buf[:, 512:1024], xh[:, 0, :]]
        tmp = route_buf[:, 1024:1536]
        nxT = [xhT[:, i, :, :] for i in range(2)]
        vr = route_buf[:, 1536:1664]
        er = route_buf[:, 1664:1760]
        sg = route_buf[:, 1760:1856]
        oh = [[GW[:, 0, 128 * i + 64 * k:128 * i + 64 * k + 64] for k in range(2)] for i in range(2)]
        Mk = [GW[:, 1, 64 * i:64 * i + 64] for i in range(2)]
        C = GW[:, 1, 128:192]
        tb = GW[:, 1, 192:256]
        junk = GW[:, 1, 256:320]
        hsig = GW[:, 1, 320:352]
        stack = [GW[:, 2, 128 * i:128 * i + 97] for i in range(2)]
        before = GW[:, 0, 256:384]
        stackT = [GW[0:97, 3, 128 * i:128 * i + 128] for i in range(2)]
        late = A[:, :]
        xg = [late[0:CAP, 512 * i:512 * i + 512] for i in range(2)]
        xe = [late[:, 1024 + 320 * i:1344 + 320 * i].rearrange("p (c t) -> p c t", c=DC) for i in range(2)]
        sl = [late[:, 1664 + 160 * i:1824 + 160 * i].rearrange("p (m t) -> p m t", m=HC) for i in range(2)]
        hT = [late[:, 1984 + 160 * i:2144 + 160 * i].rearrange("p (m t) -> p m t", m=HC) for i in range(2)]
        ysb = [late[0:CAP, 2304 + 512 * i:2816 + 512 * i] for i in range(2)]
        L = late[0:EXPERTS, 3328:3328 + CAP * REC]
        TOK = late[0:CAP, 3648:3648 + 64].bitcast(i32)
        DROW = late[0:CAP, 3712:3712 + 64].bitcast(i32)
        CW = late[0:CAP, 3776:3776 + 64]
        idx_g = late[0:CAP, 3840:3840 + 10].bitcast(i32)
        idx_s = late[0:CAP, 3856:3856 + 8].bitcast(i32)
        yfin = w13[:, 0:4, :, :, :].rearrange("p r a c h -> p (r a c h)").rearrange(
            "p (s k d) -> p s k d", s=NB, k=2)

        mv1 = small[:, 0:16].rearrange("p (s a) -> p s a", a=2)
        mv2 = small[:, 16:32].rearrange("p (s a) -> p s a", a=2)
        ve1, r1, nm1 = small[:, 32:40], small[:, 40:48], small[:, 48:56]
        ve2, r2, nm2, s2 = small[:, 56:64], small[:, 64:72], small[:, 72:80], small[:, 80:88]
        m8, i8 = small[:, 88:96], small[:, 96:104].bitcast(u32)
        idf = [small[:, 104 + 2 * i:106 + 2 * i] for i in range(2)]
        ssum, rsum = small[:, 108:109], small[:, 109:110]
        cw = [small[:, 110 + 2 * i:112 + 2 * i] for i in range(2)]
        pos = small[:, 114:116]
        slot = [small[:, 116 + 2 * i:118 + 2 * i].bitcast(i32) for i in range(2)]
        rec = [small[:, 120 + 8 * i:128 + 8 * i].rearrange("p (k a) -> p k a", k=2) for i in range(2)]
        mn, mx, nwin = small[:, 136:137], small[:, 137:138], small[:, 138:139]
        spanf, spani = small[:, 139:140], small[:, 140:141].bitcast(i32)
        st6 = small[:, 142:148]
        caps = small[0:1, 150:150 + ROUNDS]
        over = small[0:1, 170:170 + ROUNDS]
        most, nround = small[0:1, 185:186], small[0:1, 186:187]
        stdv = small[:, 192:200]
        lo8 = [small[:, 200 + 8 * i:208 + 8 * i] for i in range(2)]

        bank = [ctx.enter_context(nc.psum_tensor(f"bank{i}", [P, 512], f32)) for i in range(8)]

        edges_in, gw_in, raw_in, small_in, ws_in = (sem(s) for s in (
            "edges_in", "gw_in", "raw_in", "small_in", "ws_in"))
        x_in = [sem(f"x_in{i}") for i in range(4)]
        late_in = sem("late_in")
        consts = sem("consts")
        sentinel_out = sem("sentinel_out")
        dve_chain = sem("dve_chain")
        act_chain = sem("act_chain")
        pool_chain = sem("pool_chain")
        edge_prepped = sem("edge_prepped")
        edges_transposed = sem("edges_transposed")
        edges_ready = sem("edges_ready")
        rounds_ready = sem("rounds_ready")
        raw_transposed = sem("raw_transposed")
        raw_evac = sem("raw_evac")
        wsb_ready = sem("wsb_ready")
        sums_done = sem("sums_done")
        stats_ready = sem("stats_ready")
        std_ready = sem("std_ready")
        xh_ready = sem("xh_ready")
        xhT_ps = sem("xhT_ps")
        xhT_ready = sem("xhT_ready")
        hw_ps = sem("hw_ps")
        hw_ready = sem("hw_ready")
        lo_copied = sem("lo_copied")
        osl_ready = sem("osl_ready")
        m_ready = sem("m_ready")
        quad_done = [sem("first_quad_done"), sem("second_quad_done")]
        a_chain = sem("a_chain")
        win_chain = sem("win_chain")
        at_ps = sem("at_ps")
        at_act = sem("at_act")
        at_dve = sem("at_dve")
        out_ps = sem("out_ps")
        x1_ready = sem("x1_ready")
        mv1_ready, mv2_ready, r1_ready, r2_ready = (sem(s) for s in (
            "mv1_ready", "mv2_ready", "r1_ready", "r2_ready"))
        xt_ready, nx_ready = sem("xt_ready"), sem("nx_ready")
        nx_out = [sem(f"nx_out{i}") for i in range(2)]
        nxT_ps, nxT_ready = sem("nxT_ps"), sem("nxT_ready")
        route_ps, vr_ready, er_ready = sem("route_ps"), sem("vr_ready"), sem("er_ready")
        stack_ready, rank_ps, stackT_ready, rank_read = (sem(s) for s in (
            "stack_ready", "rank_ps", "stackT_ready", "rank_read"))
        z_ps, z_added = sem("z_ps"), sem("z_added")
        rec_ready = sem("rec_ready")
        rec_out = [sem(f"rec_out{i}") for i in range(2)]
        count_ready, count_ps = sem("count_ready"), sem("count_ps")
        tokens_ready = sem("tokens_ready")
        xg_clear = sem("xg_clear")
        w_in = [sem(f"w_in{i}") for i in range(RING)]
        list_in, list_ps, list_ready = sem("list_in"), sem("list_ps"), sem("list_ready")
        list_tok = sem("list_tok")
        idx_copied = sem("idx_copied")
        xg_in = [sem(f"xg_in{i}") for i in range(2)]
        xe_ps, xe_ready, h_ps, sl_ready, hT_ready, y_ps, y_ready = (sem(s) for s in (
            "xe_ps", "xe_ready", "h_ps", "sl_ready", "hT_ready", "y_ps", "y_ready"))
        y_out = [sem(f"y_out{i}") for i in range(2)]
        fin_in = [sem(f"fin_in{i}") for i in range(NB)]
        fin_ready = sem("fin_ready")
        out_done = sem("out_done")
        held = sem("held")

        def hold(engine):
            engine.sem_inc(held, 1)

        W1v = W1.rearrange("e (p c) h -> e p (c h)", c=DC)
        W3v = W3.rearrange("e (p c) h -> e p (c h)", c=DC)
        W2v = W2.rearrange("e (m p) d -> e p m d", p=P)
        block = ctx.enter_context(nc.Block())

        @block.sync
        def _(sp):
            edge_view = [a.rearrange("(t p) -> t p", p=P) for a in (dst, src, ew)]
            for to, a in zip((edge_dst, edge_src, edge_w), edge_view):
                sp.dma_start(to, a).then_inc(edges_in, 16)
            xv = x.rearrange("(b p) d -> p b d", p=P)
            for i in range(4):
                sp.dma_start(X[:, 2 * i:2 * i + 2, :], xv[:, 2 * i:2 * i + 2, :]).then_inc(x_in[i], 16)
            sp.dma_start(GW[:, :, :], W.rearrange("(p c) n -> p c n", c=DC)).then_inc(gw_in, 16)
            v3 = "e (c d) -> e c d"
            for to, a in ((raw_wg, Wg), (raw_g, gamma), (raw_b, beta)):
                sp.dma_start(to, a.rearrange(v3, c=4)).then_inc(raw_in, 16)
            sp.dma_start(raw_b13[:, 0:2, :], b1.rearrange(v3, c=HC)).then_inc(raw_in, 16)
            sp.dma_start(raw_b13[:, 2:4, :], b3.rearrange(v3, c=HC)).then_inc(raw_in, 16)
            sp.dma_start(gs4[:, 0, :], gs.rearrange("(p c) -> p c", c=DC)).then_inc(small_in, 16)
            sp.dma_start(gs4[:, 1, :], bs.rearrange("(p c) -> p c", c=DC)).then_inc(small_in, 16)
            sp.dma_start(bc[:, 0:64], bg.partition_broadcast(P)).then_inc(small_in, 16)
            sp.dma_start(bc[:, 64:96], bs1.partition_broadcast(P)).then_inc(small_in, 16)
            sp.dma_start(bc[:, 96:128], bs3.partition_broadcast(P)).then_inc(small_in, 16)
            sp.dma_start(Ws[:, :, 0:32], Ws1.rearrange("(p c) n -> p c n", c=DC)).then_inc(ws_in, 16)
            sp.dma_start(Ws[:, :, 32:64], Ws3.rearrange("(p c) n -> p c n", c=DC)).then_inc(ws_in, 16)
            sp.wait_ge(consts, 6)
            sp.dma_start(slots.rearrange("(p n) r -> p (n r)", p=P), sentinel).then_inc(sentinel_out, 16)

            def load_expert(e, u):
                sp.dma_start(w13[:, u, 0, :, :].rearrange("p c h -> p (c h)"), W1v[e]).then_inc(w_in[u], 16)
                sp.dma_start(w13[:, u, 1, :, :].rearrange("p c h -> p (c h)"), W3v[e]).then_inc(w_in[u], 16)
                sp.dma_start(w2[:, u, :, :], W2v[e]).then_inc(w_in[u], 16)

            for u in range(RING):
                load_expert(u, u)
            sp.wait_ge(edges_ready, 3)
            sp.dma_start(biasB, bias.partition_broadcast(P)).then_inc(late_in, 16)
            sp.dma_start(stackB[0:64, :], b2).then_inc(late_in, 16)
            sp.dma_start(stackB[64:96, :], Ws2).then_inc(late_in, 16)
            sp.dma_start(stackB[96:97, :], bs2.unsqueeze(0)).then_inc(late_in, 16)
            for s in range(NB):
                sp.wait_ge(nx_ready, s + 1)
                sp.dma_start(nx_rows[s * P:(s + 1) * P, :], nx[s % 2]).then_inc(nx_out[s % 2], 16)
            for i in range(2):
                sp.wait_ge(rec_out[i], 32 * NB // 2)
            sp.wait_ge(tokens_ready, 1)
            R2 = sp.value_load(rounds_sb[0:1, 1:2], min_val=1, max_val=ROUNDS)
            lists = slots.rearrange("(e n) r -> e (n r)", e=EXPERTS)
            with sp.Fori(0, R2) as r:
                sp.dma_start(L, lists[:, ds(r * (CAP * REC), CAP * REC)]).then_inc(list_in, 16)
                with sp.Fori(0, GROUPS - 1) as g:
                    for u in range(RING):
                        used = sp.snap(r * EXPERTS + g * RING + (u + 1))
                        e = sp.snap(g * RING + (RING + u))
                        sp.wait_ge(y_ps, used)
                        w = W1.rearrange("e (p c) h -> e p (c h)", c=DC)
                        load_expert(e, u)
                with sp.If(r + 1 < R2):
                    for u in range(RING):
                        used = sp.snap(r * EXPERTS + (EXPERTS - RING + u + 1))
                        sp.wait_ge(y_ps, used)
                        load_expert(u, u)
            last = sp.snap(R2 * (16 * EXPERTS // 2))
            yv = y_rows.rearrange("(k s p) d -> s p k d", k=2, p=P)
            for i in range(2):
                sp.wait_ge(y_out[i], last)
            for s in range(NB):
                sp.dma_start(yfin[:, s, :, :], yv[s]).then_inc(fin_in[s], 16)
            for s in range(NB):
                sp.wait_ge(fin_ready, s + 1)
                sp.dma_start(out[s * P:(s + 1) * P, :], X[:, s, :]).then_inc(out_done, 16)
            sp.wait_ge(out_done, 16 * NB)

        @block.gpsimd
        def _(pool):
            g = nc.gpsimd
            g.memset(ones[:, :], 1.0).then_inc(consts, 1)
            pool.wait_ge(consts, 1)
            g.affine_select(out=ident[:, :], in_=ones[:, :], pattern=[[-1, P]], compare_op=ALU.is_equal,
                            fill=0.0, base=0, channel_multiplier=1).then_inc(consts, 1)
            g.iota(iota[:, :], pattern=[[1, P]], base=0, channel_multiplier=0,
                   allow_small_or_imprecise_dtypes=True).then_inc(consts, 1)
            g.iota(tokcol[:, :], pattern=[[1, 1]], base=0, channel_multiplier=1,
                   allow_small_or_imprecise_dtypes=True).then_inc(consts, 1)
            g.memset(mhalf[:, :], -0.5).then_inc(consts, 1)
            g.memset(sentinel, NOWHERE).then_inc(consts, 1)
            pool.wait_ge(consts, 6)
            pool.wait_ge(edges_ready, 1)
            R1 = pool.value_load(rounds_sb[0:1, 0:1], min_val=1, max_val=N // WIN)
            with pool.Fori(0, R1) as r:
                with pool.Fori(0, NB // 2) as j:
                    for h in range(4):
                        at = (r * (NB // 2) + j) * 4 + h
                        g.tensor_copy(lo8[h % 2], eT[:, 1, ds(j * 32 + 8 * h, 8)]).then_inc(lo_copied, 1)
                        pool.wait_ge(lo_copied, at + 1)
                        hold(pool)
                        for k in range(8):
                            ins = g.tensor_scalar(osl[:, h % 2, k, :], iota[:, :], lo8[h % 2][:, k:k + 1], None, ALU.is_equal)
                        ins.then_inc(osl_ready, 1)
                        pool.wait_ge(a_chain, at * 8 + 1)
                        hold(pool)
            pool_n = [0]

            def link(ins):
                pool_n[0] += 1
                ins.then_inc(pool_chain, 1)
                pool.wait_ge(pool_chain, pool_n[0])

            def scatter_records(s):
                pool.wait_ge(rec_ready, s + 1)
                if s == 0:
                    pool.wait_ge(sentinel_out, 16)
                for k in range(2):
                    g.indirect_dma_start(slots, bass.IndirectOffsetOnAxis(ap=slot[s % 2][:, k:k + 1], axis=0),
                                         rec[s % 2][:, k, :], None).then_inc(rec_out[s % 2], 16)

            pool.wait_ge(edges_ready, 3)
            link(g.affine_select(out=before, in_=ones[:, :], pattern=[[1, P]], compare_op=ALU.is_gt,
                                 fill=0.0, base=0, channel_multiplier=-1))
            for s in range(NB + 2):
                if s < NB:
                    pool.wait_ge(mv1_ready, s + 1)
                    c = slice(s, s + 1)
                    link(g.tensor_scalar(ve1[:, c], mv1[:, s, 1:2], EPS, None, ALU.add))
                    link(g.tensor_tensor(r1[:, c], ve1[:, c], mhalf[:, :], ALU.pow))
                    link(g.tensor_tensor(nm1[:, c], mv1[:, s, 0:1], r1[:, c], ALU.mult))
                    g.tensor_scalar(nm1[:, c], nm1[:, c], -1.0, None, ALU.mult).then_inc(r1_ready, 1)
                if s >= 2:
                    scatter_records(s - 2)
                if s < NB:
                    pool.wait_ge(mv2_ready, s + 1)
                    link(g.tensor_scalar(ve2[:, c], mv2[:, s, 1:2], EPS, None, ALU.add))
                    link(g.tensor_tensor(r2[:, c], ve2[:, c], mhalf[:, :], ALU.pow))
                    link(g.tensor_tensor(s2[:, c], ve2[:, c], r2[:, c], ALU.mult))
                    link(g.tensor_tensor(nm2[:, c], mv2[:, s, 0:1], r2[:, c], ALU.mult))
                    g.tensor_scalar(nm2[:, c], nm2[:, c], -1.0, None, ALU.mult).then_inc(r2_ready, 1)
            pool.wait_ge(at_ps, 2 * NB)
            g.memset(xg[0], 0.0).then_inc(xg_clear, 1)
            g.memset(xg[1], 0.0).then_inc(xg_clear, 1)
            pool.wait_ge(xg_clear, 2)
            pool.wait_ge(nx_out[0], 16 * NB // 2)
            pool.wait_ge(nx_out[1], 16 * NB // 2)
            pool.wait_ge(tokens_ready, 1)
            R2 = pool.value_load(rounds_sb[0:1, 1:2], min_val=1, max_val=ROUNDS)

            def gather(col, b):
                g.indirect_dma_start(xg[b], None, nx_rows, bass.IndirectOffsetOnAxis(ap=idx_g[:, col:col + 1], axis=0),
                                     bounds_check=N - 1, oob_is_err=False).then_inc(xg_in[b], 16)

            def scatter(u, count):
                pool.wait_ge(y_ready, count)
                hold(pool)
                g.indirect_dma_start(y_rows, bass.IndirectOffsetOnAxis(ap=idx_s[:, u:u + 1], axis=0), ysb[u % 2], None,
                                     bounds_check=2 * N - 1, oob_is_err=False).then_inc(y_out[u % 2], 16)

            with pool.Fori(0, R2) as r:
                pool.wait_ge(list_ready, r + 1)
                hold(pool)
                g.tensor_copy(idx_g[:, 0:2], TOK[:, 0:2]).then_inc(idx_copied, 1)
                pool.wait_ge(idx_copied, r * (2 * GROUPS + 1) + 1)
                hold(pool)
                gather(0, 0)
                gather(1, 1)

                def group(gi, first, last):
                    n = RING if last else RING + 2
                    base = r * EXPERTS + gi * RING
                    pool.wait_ge(xg_in[0], (r * (EXPERTS // 2) + gi * (RING // 2) + 1) * 16)
                    pool.wait_ge(xg_in[1], (r * (EXPERTS // 2) + gi * (RING // 2) + 1) * 16)
                    hold(pool)
                    g.tensor_copy(idx_g[:, 0:n], TOK[:, ds(gi * RING, n)]).then_inc(idx_copied, 1)
                    if not first:
                        pool.wait_ge(y_out[0], (r * (EXPERTS // 2) + gi * (RING // 2)) * 16)
                        pool.wait_ge(y_out[1], (r * (EXPERTS // 2) + gi * (RING // 2)) * 16)
                        hold(pool)
                    g.tensor_copy(idx_s[:, :], DROW[:, ds(gi * RING, RING)]).then_inc(idx_copied, 1)
                    pool.wait_ge(idx_copied, r * (2 * GROUPS + 1) + gi * 2 + 3)
                    hold(pool)
                    for u in range(RING):
                        if not (last and u >= RING - 2):
                            pool.wait_ge(xe_ps, base + u + 1)
                            hold(pool)
                            gather(u + 2, u % 2)
                        if u:
                            scatter(u - 1, base + u)
                    scatter(RING - 1, base + RING)

                group(0, True, False)
                with pool.Fori(1, GROUPS - 1) as gi:
                    group(gi, False, False)
                group(GROUPS - 1, False, True)
                for i in range(2):
                    pool.wait_ge(y_out[i], (r + 1) * (16 * EXPERTS // 2))

        @block.scalar
        def _(act):
            a = nc.scalar
            a.memzero(A[:, :]).then_inc(a_chain, 1)
            act.wait_ge(raw_transposed, 1)
            a.copy(R[:, :, 0:64], bank[2][:, 0:256].rearrange("p (c e) -> p c e", c=DC)).then_inc(raw_evac, 1)
            a.copy(gT[:, :, :].rearrange("p c e -> p (c e)"), bank[2][:, 256:512]).then_inc(raw_evac, 1)
            act.wait_ge(raw_transposed, 2)
            a.copy(bT[:, :, :].rearrange("p c e -> p (c e)"), bank[3][:, 0:256]).then_inc(raw_evac, 1)
            a.copy(b13T[:, :, :, :].rearrange("p a m e -> p (a m e)"), bank[3][:, 256:512]).then_inc(raw_evac, 1)
            act.wait_ge(stats_ready, 1)
            a.activation(stdv, mv[:, :, 1], ACT.Sqrt, bias=eps_c[:, :]).then_inc(std_ready, 1)
            act.wait_ge(sentinel_out, 16)
            with act.Fori(0, NB // 2) as j:
                for u in range(2):
                    act.wait_ge(xhT_ps, j * 2 + u + 1)
                    a.copy(xhT[:, u, :, :].rearrange("p c n -> p (c n)"), bank[4 + u][:, :]).then_inc(xhT_ready, 1)
                    act.wait_ge(hw_ps, j * 2 + u + 1)
                    a.copy(HW[:, ds(j * 2 + u, 1), :].rearrange("p a n -> p (a n)"), bank[6 + u][:, :]).then_inc(hw_ready, 1)

            def at_half(s):
                act.wait_ge(at_ps, 2 * s + 1)
                a.copy(AT[:, s % 2, 0:4, :].rearrange("p k n -> p (k n)"), bank[2 * (s % 2)][:, :]).then_inc(at_act, 1)

            at_half(0)
            for s in range(NB + 2):
                if s + 1 < NB:
                    if s >= 1:
                        act.wait_ge(out_ps, s)
                    at_half(s + 1)
                if s >= 2:
                    t = s - 2
                    act.wait_ge(vr_ready, t + 1)
                    a.activation(er, er, ACT.Exp, scale=-1.0).then_inc(er_ready, 1)
                if 1 <= s <= NB:
                    t = s - 1
                    act.wait_ge(nxT_ps, t + 1)
                    a.copy(nxT[t % 2].rearrange("p c n -> p (c n)"), bank[6][:, :]).then_inc(nxT_ready, 1)
                if s < NB:
                    act.wait_ge(r1_ready, s + 1)
                    a.activation(xt, X[:, s, :], ACT.Identity, scale=r1[:, s:s + 1], bias=nm1[:, s:s + 1]).then_inc(xt_ready, 1)
                    act.wait_ge(xt_ready, s + 1)
                    act.wait_ge(r2_ready, s + 1)
                    if s >= 2:
                        act.wait_ge(nx_out[s % 2], 16 * (s // 2))
                        act.wait_ge(nxT_ps, s - 1)
                    a.activation(nx[s % 2], xt, ACT.Identity, scale=r2[:, s:s + 1], bias=nm2[:, s:s + 1]).then_inc(nx_ready, 1)
            act.wait_ge(tokens_ready, 1)
            R2 = act.value_load(rounds_sb[0:1, 1:2], min_val=1, max_val=ROUNDS)
            with act.Fori(0, R2) as r:
                def group(g, first):
                    base = r * EXPERTS + g * RING

                    def silu(u):
                        act.wait_ge(h_ps, base + u + 1)
                        for m in range(HC):
                            ins = a.activation(sl[u % 2][:, m, :], bank[2 + u % 2][:, m * CAP:(m + 1) * CAP], ACT.Silu,
                                               bias=b13T[:, 0, m, ds(g * RING + u, 1)])
                        ins.then_inc(sl_ready, 1)

                    def result(u):
                        act.wait_ge(y_ps, base + u + 1)
                        if not first or u >= 2:
                            act.wait_ge(y_out[u % 2], (r * (EXPERTS // 2) + g * (RING // 2) + u // 2) * 16)
                        a.activation(ysb[u % 2], bank[6 + u % 2][0:CAP, :], ACT.Copy,
                                     scale=CW[:, ds(g * RING + u, 1)]).then_inc(y_ready, 1)

                    for u in range(RING):
                        silu(u)
                        if u:
                            result(u - 1)
                    result(RING - 1)

                act.wait_ge(list_ready, r + 1)
                group(0, True)
                with act.Fori(1, GROUPS) as g:
                    group(g, False)

        @block.vector
        def _(dve):
            v = nc.vector
            chain = [0]

            def link(ins):
                chain[0] += 1
                ins.then_inc(dve_chain, 1)
                dve.wait_ge(dve_chain, chain[0])

            link(v.memset(eps_c[:, :], EPS))
            dve.wait_ge(edges_in, 48)
            link(v.tensor_scalar(d8, edge_dst, 3, None, ALU.arith_shift_left))
            link(v.tensor_scalar(shi, edge_src, 7, None, ALU.arith_shift_right))
            link(v.tensor_scalar(slo, edge_src, P - 1, None, ALU.bitwise_and))
            link(v.tensor_tensor(key, d8, shi, ALU.add))
            link(v.tensor_copy(slof, slo))
            link(v.tensor_reduce(mn, d8, AX, ALU.min))
            link(v.tensor_reduce(mx, d8, AX, ALU.max))
            link(v.tensor_scalar(key, key, mn, None, ALU.subtract))
            link(v.tensor_tensor(spani, mx, mn, ALU.subtract))
            link(v.tensor_scalar(spani, spani, 7, None, ALU.arith_shift_right))
            v.tensor_scalar(nwin, spani, 1.0, None, ALU.add).then_inc(edge_prepped, 1)
            dve.wait_ge(edges_transposed, 1)
            link(v.tensor_copy(eT[:, :, :].rearrange("p a t -> p (a t)"), bank[0][:, 0:3 * P]))
            link(v.tensor_copy(wrow[:, :], bank[1][0:1, 0:2 * P]))
            link(v.tensor_reduce(rounds_sb[0:1, 0:1], wrow[:, P:2 * P], AX, ALU.max))
            v.tensor_copy(wbase, wrow[:, 0:P]).then_inc(edges_ready, 1)
            for b in range(NB):
                if b % 2 == 0:
                    dve.wait_ge(x_in[b // 2], 16)
                link(v.bn_stats(stats[:, 6 * b:6 * b + 6], X[:, b, :]))
                ins = v.bn_aggr(mv[:, b, :], stats[:, 6 * b:6 * b + 6])
                if b < NB - 1:
                    link(ins)
                else:
                    ins.then_inc(stats_ready, 1)
            dve.wait_ge(small_in, 80)
            dve.wait_ge(ws_in, 32)
            for c in range(DC):
                link(v.tensor_scalar(R[:, c, 64:128], Ws[:, c, :], gs4[:, 0, c:c + 1], None, ALU.mult))
                ins = v.tensor_scalar(Wsb[:, c, :], Ws[:, c, :], gs4[:, 1, c:c + 1], None, ALU.mult)
                if c < DC - 1:
                    link(ins)
            ins.then_inc(wsb_ready, 1)
            dve.wait_ge(sums_done, 1)
            link(v.tensor_copy(rowWg[:, :], bank[1][:, 256:320]))
            link(v.tensor_tensor(bc[:, 64:128], bc[:, 64:128], bank[1][:, 320:384], ALU.add))
            dve.wait_ge(std_ready, 1)
            link(v.reciprocal(rstd[:, :], stdv))
            dve.wait_ge(edges_ready, 1)
            R1 = dve.value_load(rounds_sb[0:1, 0:1], min_val=1, max_val=N // WIN)

            def sum_pair(r, j, with_x):
                if with_x:
                    for u in range(2):
                        b = j * 2 + u
                        v.tensor_scalar(xh[:, u, :], X[:, ds(b, 1), :].rearrange("p a n -> p (a n)"),
                                        mv[:, ds(b, 1), 0], rstd[:, ds(b, 1)],
                                        ALU.subtract, ALU.mult).then_inc(xh_ready, 1)
                done = dve.snap((r * (NB // 2) + j) * 4)
                added = dve.snap(done * (2 * QUAD))

                def sums(q):
                    dve.wait_ge(quad_done[q % 2], done + (q // 2 + 1))
                    _, at = nc.values_load_multi_w_load_instructions(
                        wbase[0:1, ds(j * 32 + QUAD * q, QUAD)], engines=[mybir.EngineType.DVE],
                        min_val=0, max_val=8 * N, skip_runtime_bounds_check_because="DVE bounded them by min and the keys are >= 0")
                    for k in range(QUAD):
                        to = A[:, ds(at[k], P)]
                        dve.wait_ge(a_chain, added + (QUAD * q + k + 1))
                        v.tensor_tensor(to, to, bank[2 + q % 2][:, k * P:(k + 1) * P], ALU.add).then_inc(a_chain, 1)

                for q in range(8):
                    for k in range(QUAD):
                        t = j * 32 + QUAD * q + k
                        ins = v.tensor_scalar(M[:, q % 2, k, :], iota[:, :], eT[:, 0, ds(t, 1)], eT[:, 2, ds(t, 1)],
                                              ALU.is_equal, ALU.mult)
                    ins.then_inc(m_ready, 1)
                    if q:
                        sums(q - 1)
                sums(7)

            with dve.Fori(0, NB // 2) as j:
                sum_pair(0, j, True)
            more = dve.snap(R1)
            with dve.If(more > 1):
                with dve.Fori(1, R1) as r:
                    w = dve.snap(r * 3)
                    v.tensor_scalar(eT[:, 0, :], eT[:, 0, :], float(P), None, ALU.subtract).then_inc(win_chain, 1)
                    v.tensor_scalar(wrow[:, 0:P], wrow[:, 0:P], float(P), None, ALU.add).then_inc(win_chain, 1)
                    dve.wait_ge(win_chain, w - 1)
                    v.tensor_scalar(wbase, wrow[:, 0:P], float(8 * N), None, ALU.min).then_inc(win_chain, 1)
                    dve.wait_ge(win_chain, w)
                    hold(dve)
                    with dve.Fori(0, NB // 2) as j:
                        sum_pair(r, j, False)
            dve.wait_ge(a_chain, R1 * TILES + 1)
            dve.wait_ge(hw_ps, NB)
            v.memset(C, 0.0).then_inc(edges_ready, 1)
            dve.wait_ge(edges_ready, 2)
            v.memset(junk, 0.0).then_inc(edges_ready, 1)

            def at_half(s):
                dve.wait_ge(at_ps, 2 * s + 2)
                v.tensor_copy(AT[:, s % 2, 4:8, :].rearrange("p k n -> p (k n)"), bank[2 * (s % 2) + 1][:, :]).then_inc(at_dve, 1)

            def relu_add(s):
                dve.wait_ge(out_ps, s + 1)
                if s == 0:
                    dve.wait_ge(late_in, 64)
                link(v.tensor_tensor(tmp, bank[4 + s % 2][:, :], biasB, ALU.add))
                v.scalar_tensor_tensor(X[:, s, :], tmp, 0.0, X[:, s, :], ALU.max, ALU.add).then_inc(x1_ready, 1)
                dve.wait_ge(x1_ready, s + 1)
                link(v.bn_stats(st6, X[:, s, :]))
                v.bn_aggr(mv1[:, s, :], st6).then_inc(mv1_ready, 1)

            def route(t):
                i = t % 2
                dve.wait_ge(route_ps, t + 1)
                link(v.scalar_tensor_tensor(tb, rowWg[:, :], mv2[:, t, 0:1], bc[:, 0:64], ALU.mult, ALU.add))
                link(v.scalar_tensor_tensor(vr[:, 0:64], bank[7][:, 0:64], s2[:, t:t + 1], tb, ALU.mult, ALU.add))
                link(v.tensor_tensor(vr[:, 64:128], bank[7][:, 64:128], bc[:, 64:128], ALU.add))
                v.tensor_scalar(er, vr[:, 0:96], -87.0, None, ALU.max).then_inc(vr_ready, 1)
                dve.wait_ge(er_ready, t + 1)
                link(v.tensor_scalar(er, er, 1.0, None, ALU.add))
                link(v.reciprocal(sg, er))
                link(v.max(m8, sg[:, 0:64]))
                link(v.max_index(i8, m8, sg[:, 0:64]))
                link(v.tensor_copy(idf[i], i8[:, 0:2]))
                link(v.tensor_tensor(ssum, m8[:, 0:1], m8[:, 1:2], ALU.add))
                link(v.reciprocal(rsum, ssum))
                link(v.tensor_scalar(cw[i], m8[:, 0:2], rsum, None, ALU.mult))
                for k in range(2):
                    link(v.tensor_scalar(oh[i][k], iota[:, 0:64], idf[i][:, k:k + 1], None, ALU.is_equal))
                link(v.tensor_scalar(tb, oh[i][0], cw[i][:, 0:1], None, ALU.mult))
                link(v.scalar_tensor_tensor(stack[i][:, 0:64], oh[i][1], cw[i][:, 1:2], tb, ALU.mult, ALU.add))
                link(v.tensor_tensor(Mk[i], oh[i][0], oh[i][1], ALU.add))
                link(v.tensor_tensor(hsig, vr[:, 64:96], sg[:, 64:96], ALU.mult))
                link(v.tensor_tensor(stack[i][:, 64:96], hsig, vr[:, 96:128], ALU.mult))
                v.memset(stack[i][:, 96:97], 1.0).then_inc(stack_ready, 1)

            def rank(t):
                i = t % 2
                dve.wait_ge(rank_ps, t + 1)
                v.tensor_copy(stackT[i], bank[7][0:97, 0:P]).then_inc(stackT_ready, 1)
                for k in range(2):
                    link(v.tensor_tensor_reduce(out=junk, in0=oh[i][k], in1=bank[7][:, 128:192], scale=1.0, scalar=0.0,
                                                op0=ALU.mult, op1=ALU.add, accum_out=pos[:, k:k + 1]))
                if t >= 2:
                    dve.wait_ge(rec_out[i], 32 * (t // 2))
                link(v.scalar_tensor_tensor(slot[i], idf[i], float(LIST), pos, ALU.mult, ALU.add))
                for k in range(2):
                    link(v.tensor_scalar(rec[i][:, k, 0:1], tokcol[:, :], float(P * t), None, ALU.add))
                    link(v.tensor_scalar(rec[i][:, k, 1:2], tokcol[:, :], float(P * t + N * k), None, ALU.add))
                    link(v.tensor_copy(rec[i][:, k, 2:3], cw[i][:, k:k + 1]))
                    link(v.memset(rec[i][:, k, 3:4], 0.0))
                v.tensor_tensor(C, C, Mk[i], ALU.add).then_inc(rec_ready, 1)
                dve.wait_ge(rec_ready, t + 1)

            at_half(0)
            for s in range(NB + 3):
                if s + 1 < NB:
                    if s >= 1:
                        dve.wait_ge(out_ps, s)
                    at_half(s + 1)
                if s >= 3:
                    dve.wait_ge(z_ps, s - 2)
                    v.tensor_tensor(X[:, s - 3, :], X[:, s - 3, :], bank[6][:, :], ALU.add).then_inc(z_added, 1)
                if 2 <= s < NB + 2:
                    route(s - 2)
                if s < NB:
                    relu_add(s)
                if 2 <= s < NB + 2:
                    rank(s - 2)
                    if s == NB + 1:
                        link(v.tensor_scalar(caps, iota[0:1, 0:ROUNDS], float(CAP), None, ALU.mult))
                        dve.wait_ge(count_ps, 1)
                        link(v.tensor_reduce(most, bank[5][0:1, 0:64], AX, ALU.max))
                        link(v.tensor_scalar(over, caps, most, None, ALU.is_lt))
                        link(v.tensor_reduce(nround, over, AX, ALU.add))
                        v.tensor_copy(rounds_sb[0:1, 1:2], nround).then_inc(tokens_ready, 1)
                if s < NB:
                    dve.wait_ge(xt_ready, s + 1)
                    link(v.bn_stats(st6, xt))
                    v.bn_aggr(mv2[:, s, :], st6).then_inc(mv2_ready, 1)

            dve.wait_ge(tokens_ready, 1)
            R2 = dve.value_load(rounds_sb[0:1, 1:2], min_val=1, max_val=ROUNDS)
            with dve.Fori(0, R2) as r:
                dve.wait_ge(list_ps, r + 1)
                v.tensor_copy(TOK, bank[6][0:CAP, 0:64])
                v.tensor_copy(DROW, bank[6][0:CAP, 64:128])
                v.tensor_copy(CW, bank[6][0:CAP, 128:192]).then_inc(list_ready, 1)

                def rows(gi, u, count):
                    dve.wait_ge(xe_ps, count)
                    b = u % 2
                    for c in range(DC):
                        e = gi * RING + u
                        ins = v.tensor_scalar(xe[b][:, c, :], bank[b][:, c * CAP:(c + 1) * CAP], gT[:, c, ds(e, 1)],
                                              bT[:, c, ds(e, 1)], ALU.mult, ALU.add)
                    ins.then_inc(xe_ready, 1)

                rows(0, 0, r * EXPERTS + 1)

                def group(gi, last):
                    base = r * EXPERTS + gi * RING
                    for u in range(RING):
                        if not (last and u == RING - 1):
                            rows(gi, u + 1, base + u + 2)
                        dve.wait_ge(sl_ready, base + u + 1)
                        for m in range(HC):
                            ins = v.scalar_tensor_tensor(hT[u % 2][:, m, :], bank[4 + u % 2][:, m * CAP:(m + 1) * CAP],
                                                         b13T[:, 1, m, ds(gi * RING + u, 1)], sl[u % 2][:, m, :],
                                                         ALU.add, ALU.mult)
                        ins.then_inc(hT_ready, 1)

                with dve.Fori(0, GROUPS - 1) as gi:
                    group(gi, False)
                group(GROUPS - 1, True)
                for i in range(2):
                    dve.wait_ge(y_out[i], (r + 1) * (16 * EXPERTS // 2))
            for s in range(NB):
                dve.wait_ge(fin_in[s], 16)
                link(v.tensor_tensor(X[:, s, :], X[:, s, :], yfin[:, s, 0, :], ALU.add))
                v.tensor_tensor(X[:, s, :], X[:, s, :], yfin[:, s, 1, :], ALU.add).then_inc(fin_ready, 1)

        @block.tensor
        def _(pe):
            t = nc.tensor
            pe.wait_ge(consts, 5)
            pe.wait_ge(edge_prepped, 1)
            t.transpose(bank[0][:, 0:P], key, ident[:, :])
            t.transpose(bank[0][:, P:2 * P], slof, ident[:, :])
            t.transpose(bank[0][:, 2 * P:3 * P], edge_w, ident[:, :])
            t.matmul(bank[1][0:1, 0:P], mn, ident[:, :], start=True, stop=True)
            t.matmul(bank[1][0:1, P:2 * P], nwin, ident[:, :], start=True, stop=True).then_inc(edges_transposed, 1)
            pe.wait_ge(raw_in, 80)
            id64 = ident[0:64, 0:64]
            for i, raw in enumerate((raw_wg, raw_g, raw_b)):
                flat = raw.rearrange("e c d -> e (c d)")
                for c in range(DC):
                    ins = t.transpose(bank[2 + i // 2][:, (i % 2) * 256 + 64 * c:(i % 2) * 256 + 64 * c + 64],
                                      flat[:, c:c + DC * (P - 1) + 1:DC], id64)
                if i == 1:
                    ins.then_inc(raw_transposed, 1)
            for c in range(2 * HC):
                ins = t.transpose(bank[3][:, 256 + 64 * c:320 + 64 * c], raw_b13[:, c, :], id64)
            ins.then_inc(raw_transposed, 1)
            pe.wait_ge(raw_evac, 4)
            pe.wait_ge(wsb_ready, 1)
            for c in range(DC):
                t.matmul(bank[1][:, 256:320], ones[:, :], R[:, c, 0:64], start=(c == 0), stop=(c == DC - 1))
            for c in range(DC):
                ins = t.matmul(bank[1][:, 320:384], ones[:, :], Wsb[:, c, :], start=(c == 0), stop=(c == DC - 1))
            ins.then_inc(sums_done, 1)
            pe.wait_ge(edges_ready, 1)
            R1 = pe.value_load(rounds_sb[0:1, 0:1], min_val=1, max_val=N // WIN)
            pe.wait_ge(gw_in, 16)

            def pair(r, j, with_x):
                half = pe.snap((r * (NB // 2) + j) * 4)
                quad = pe.snap(half * 2)
                for u in range(2):
                    if with_x:
                        pe.wait_ge(xh_ready, j * 2 + u + 1)
                        for c in range(DC):
                            ins = t.transpose(bank[4 + u][:, c * P:(c + 1) * P], xh[:, u, c:c + DC * (P - 1) + 1:DC], ident[:, :])
                        ins.then_inc(xhT_ps, 1)
                    for q in range(4 * u, 4 * u + 4):
                        if q % 2 == 0:
                            pe.wait_ge(osl_ready, half + (q // 2 + 1))
                        pe.wait_ge(m_ready, quad + (q + 1))
                        for k in range(QUAD):
                            ins = t.matmul(bank[2 + q % 2][:, k * P:(k + 1) * P], osl[:, (q // 2) % 2, (q % 2) * QUAD + k, :],
                                           M[:, q % 2, k, :], start=True, stop=True)
                        ins.then_inc(quad_done[q % 2], 1)
                    if with_x:
                        pe.wait_ge(xhT_ready, j * 2 + u + 1)
                        for c in range(DC):
                            ins = t.matmul(bank[6 + u][:, :], xhT[:, u, c, :], GW[:, c, :], start=(c == 0), stop=(c == DC - 1))
                        ins.then_inc(hw_ps, 1)

            with pe.Fori(0, NB // 2) as j:
                pair(0, j, True)
            with pe.If(R1 > 1):
                with pe.Fori(1, R1) as r:
                    with pe.Fori(0, NB // 2) as j:
                        pair(r, j, False)
            pe.wait_ge(edges_ready, 3)
            pe.wait_ge(hw_ready, NB)
            A3 = A[:, :].rearrange("p (n s) -> p n s", s=8)

            def transpose_a(s):
                for k in range(NB):
                    ins = t.transpose(bank[2 * (s % 2) + k // 4][:, (k % 4) * P:(k % 4 + 1) * P], A3[:, k * P:(k + 1) * P, s], ident[:, :])
                    if k % 4 == 3:
                        ins.then_inc(at_ps, 1)

            def sum_messages(s, ks):
                if ks[0] == 0:
                    pe.wait_ge(at_act, s + 1)
                    pe.wait_ge(at_dve, s + 1)
                    if s >= 2:
                        pe.wait_ge(x1_ready, s - 1)
                for k in ks:
                    ins = t.matmul(bank[4 + s % 2][:, :], AT[:, s % 2, k, :], HW[:, k, :], start=(k == 0), stop=(k == NB - 1))
                if ks[-1] == NB - 1:
                    ins.then_inc(out_ps, 1)

            def transpose_nx(b):
                pe.wait_ge(nx_ready, b + 1)
                if b >= 2:
                    pe.wait_ge(z_added, b - 1)
                for c in range(DC):
                    ins = t.transpose(bank[6][:, c * P:(c + 1) * P], nx[b % 2][:, c:c + DC * (P - 1) + 1:DC], ident[:, :])
                ins.then_inc(nxT_ps, 1)

            def route(b):
                pe.wait_ge(nxT_ready, b + 1)
                if b >= 1:
                    pe.wait_ge(rec_ready, b)
                for c in range(DC):
                    ins = t.matmul(bank[7][:, 0:P], nxT[b % 2][:, c, :], R[:, c, :], start=(c == 0), stop=(c == DC - 1))
                ins.then_inc(route_ps, 1)

            def rank(b):
                pe.wait_ge(stack_ready, b + 1)
                t.transpose(bank[7][0:97, 0:P], stack[b % 2], ident[:, :])
                t.matmul(bank[7][:, 128:192], before, Mk[b % 2], start=True, stop=False)
                if b >= 1:
                    pe.wait_ge(rec_ready, b)
                t.matmul(bank[7][:, 128:192], ones[:, :], C, start=False, stop=True).then_inc(rank_ps, 1)

            def shared(b):
                pe.wait_ge(stackT_ready, b + 1)
                pe.wait_ge(nxT_ready, min(b + 2, NB))
                t.matmul(bank[6][:, :], stackT[b % 2], stackB, start=True, stop=True).then_inc(z_ps, 1)

            transpose_a(0)
            for s in range(NB + 3):
                if s + 1 < NB:
                    transpose_a(s + 1)
                if s < NB:
                    sum_messages(s, range(0, 4))
                if s >= 3:
                    shared(s - 3)
                if 2 <= s < NB + 2:
                    route(s - 2)
                if s < NB:
                    sum_messages(s, range(4, 8))
                if 1 <= s <= NB:
                    transpose_nx(s - 1)
                if 2 <= s < NB + 2:
                    rank(s - 2)
                    if s == NB + 1:
                        pe.wait_ge(rec_ready, NB)
                        t.matmul(bank[5][0:1, 0:64], ones[:, 0:1], C, start=True, stop=True).then_inc(count_ps, 1)

            pe.wait_ge(z_added, NB)
            pe.wait_ge(tokens_ready, 1)
            R2 = pe.value_load(rounds_sb[0:1, 1:2], min_val=1, max_val=ROUNDS)
            with pe.Fori(0, R2) as r:
                pe.wait_ge(list_in, (r + 1) * 16)
                hold(pe)
                for a in range(3):
                    ins = t.transpose(bank[6][0:CAP, 64 * a:64 * a + 64], L[:, a:a + REC * (CAP - 1) + 1:REC], ident[0:64, 0:64])
                ins.then_inc(list_ps, 1)

                def rows(u, count):
                    pe.wait_ge(xg_in[u % 2], count * 16)
                    for c in range(DC):
                        ins = t.transpose(bank[u % 2][:, c * CAP:(c + 1) * CAP], xg[u % 2][:, c:c + DC * (P - 1) + 1:DC], ident[0:CAP, 0:CAP])
                    ins.then_inc(xe_ps, 1)

                rows(0, r * (EXPERTS // 2) + 1)

                def group(gi, last):
                    base = r * EXPERTS + gi * RING
                    pairs = r * (EXPERTS // 2) + gi * (RING // 2)
                    uses = (r * GROUPS + gi + 1) * 48

                    def up(u):
                        pe.wait_ge(w_in[u], uses)
                        pe.wait_ge(xe_ready, base + u + 1)
                        for a, b in ((0, 2 + u % 2), (1, 4 + u % 2)):
                            for m in range(HC):
                                for c in range(DC):
                                    ins = t.matmul(bank[b][:, m * CAP:(m + 1) * CAP], w13[:, u, a, c, m * P:(m + 1) * P],
                                                   xe[u % 2][:, c, :], start=(c == 0), stop=(c == DC - 1))
                        ins.then_inc(h_ps, 1)

                    def down(u):
                        pe.wait_ge(hT_ready, base + u + 1)
                        for m in range(HC):
                            ins = t.matmul(bank[6 + u % 2][0:CAP, :], hT[u % 2][:, m, :], w2[:, u, m, :],
                                           start=(m == 0), stop=(m == HC - 1))
                        ins.then_inc(y_ps, 1)

                    for u in range(RING):
                        if not (last and u == RING - 1):
                            rows(u + 1, pairs + ((u + 1) // 2 + 1))
                        up(u)
                        if u:
                            down(u - 1)
                    down(RING - 1)

                with pe.Fori(0, GROUPS - 1) as gi:
                    group(gi, False)
                group(GROUPS - 1, True)
                pe.wait_ge(y_ready, (r + 1) * EXPERTS)


_INS = ['x', 'src', 'dst', 'edge_weight', 'L0_gnn_W', 'L0_gnn_bias', 'L0_ffn_Wg', 'L0_ffn_bg', 'L0_ffn_gamma',
        'L0_ffn_beta', 'L0_ffn_W1', 'L0_ffn_b1', 'L0_ffn_W3', 'L0_ffn_b3', 'L0_ffn_W2', 'L0_ffn_b2', 'L0_ffn_gs',
        'L0_ffn_bs', 'L0_ffn_Ws1', 'L0_ffn_bs1', 'L0_ffn_Ws3', 'L0_ffn_bs3', 'L0_ffn_Ws2', 'L0_ffn_bs2']


def kernel(**inputs):
    import numpy as _np
    import concourse.bacc as _bacc
    from concourse import mybir as _mybir
    from concourse.bass_utils import run_bass_kernel_spmd as _run

    nc = _bacc.Bacc("TRN2", target_bir_lowering=False, num_devices=1)
    arrays, args = {}, []
    for name in _INS:
        a = _np.ascontiguousarray(inputs[name])
        arrays[f"in_{name}_dram"] = a
        args.append(nc.dram_tensor(f"in_{name}_dram", a.shape, _mybir.dt.from_np(a.dtype), kind="ExternalInput").ap())
    out = nc.dram_tensor("out_dram", (N, D), _mybir.dt.float32, kind="ExternalOutput").ap()
    moe_gnn(nc, *args, out)
    r = _run(nc, [arrays], core_ids=[0])
    return r.results[0]["out_dram"]
```

```python
import numpy as np
import concourse.bass as bass
from concourse import mybir
from contextlib import ExitStack

N, D = 1024, 512
EDGES = 16384
EXPERTS, HID, HS = 64, 256, 32
EPS = 1e-5
P = 128
NB = N // P
DC = D // P
HC = HID // P
TILES = EDGES // P
WIN = 16
QUAD = 4
CAP = 80
ROUNDS = -(-N // CAP)
LIST = ROUNDS * CAP
REC = 4
RING = 8
GROUPS = EXPERTS // RING
XG, AHEAD = 8, 6
YS = 4
NOWHERE = 60000.0


def moe_gnn(nc, x, src, dst, ew, W, bias, Wg, bg, gamma, beta, W1, b1, W3, b3, W2, b2,
            gs, bs, Ws1, bs1, Ws3, bs3, Ws2, bs2, out):
    f32, i32, u32 = mybir.dt.float32, mybir.dt.int32, mybir.dt.uint32
    ALU = mybir.AluOpType
    ACT = mybir.ActivationFunctionType
    AX = mybir.AxisListType.X
    ds = bass.ds

    ctx = ExitStack()
    with ctx:
        def sb(name, shape, dt=f32):
            return ctx.enter_context(nc.sbuf_tensor(name, shape, dt))

        def sem(name):
            return ctx.enter_context(nc.semaphore(name))

        nx_rows = nc.dram_tensor("nx_rows", (N, D), f32).ap()
        slots = nc.dram_tensor("slots", (EXPERTS * LIST, REC), f32).ap()
        y_rows = nc.dram_tensor("y_rows", (2 * N, D), f32).ap()

        w13 = sb("w13", [P, RING, 2, DC, HID])
        w2 = sb("w2", [P, RING, HC, D])
        X = sb("X", [P, NB, D])
        A = sb("A", [P, (N + WIN) * 8])
        HW = sb("HW", [P, NB, D])
        GW = sb("GW", [P, DC, D])
        osl = sb("osl", [P, 2, 8, P])
        M = sb("M", [P, 2, QUAD, P])
        xh = sb("xh", [P, 2, D])
        xhT = sb("xhT", [P, 2, DC, P])
        AT = sb("AT", [P, 2, NB, P])
        eT = sb("eT", [P, 3, P])
        wrow = sb("wrow", [1, 2 * P])
        wbase = wrow[:, P:2 * P].bitcast(i32)
        rounds_sb = sb("rounds_sb", [1, 2], i32)
        ident = sb("ident", [P, P])
        ones = sb("ones", [P, P])
        iota = sb("iota", [P, P])
        tokcol = sb("tokcol", [P, 1])
        eps_c = sb("eps_c", [P, 1])
        mhalf = sb("mhalf", [P, 1])
        stats = sb("stats", [P, 6 * NB])
        mv = sb("mv", [P, NB, 2])
        rstd = sb("rstd", [P, NB])
        gT = sb("gT", [P, DC, EXPERTS])
        bT = sb("bT", [P, DC, EXPERTS])
        b13T = sb("b13T", [P, 2, HC, EXPERTS])
        R = sb("R", [P, DC, P])
        bc = sb("bc", [P, P])
        rowWg = sb("rowWg", [P, EXPERTS])
        gs4 = sb("gs4", [P, 2, DC])
        small = sb("small", [P, 256])

        raw_wg, raw_g, raw_b = AT[0:64, 0, 0:4, :], AT[0:64, 0, 4:8, :], AT[0:64, 1, 0:4, :]
        raw_b13 = AT[0:64, 1, 4:8, :]
        edge_src, edge_dst = xhT[:, 0, 0, :].bitcast(i32), xhT[:, 0, 1, :].bitcast(i32)
        edge_w = xhT[:, 0, 2, :]
        d8 = xhT[:, 0, 3, :].bitcast(i32)
        shi = xhT[:, 1, 0, :].bitcast(i32)
        slo = xhT[:, 1, 1, :].bitcast(i32)
        key = xhT[:, 1, 2, :]
        slof = xhT[:, 1, 3, :]
        Ws = HW[:, NB - 1, 0:4 * 64].rearrange("p (c n) -> p c n", c=DC)
        Wsb = HW[:, NB - 1, 4 * 64:8 * 64].rearrange("p (c n) -> p c n", c=DC)
        sentinel = HW[:, 0:5, :].rearrange("p b d -> p (b d)")[:, 0:EXPERTS * LIST * REC // P]
        biasB = M[:, 0, :, :].rearrange("p a b -> p (a b)")
        stackB = M[0:97, 1, :, :].rearrange("p a b -> p (a b)")
        route_buf = osl[:, :, :, :].rearrange("p a b c -> p (a b c)")
        xt = route_buf[:, 0:512]
        nx = [route_buf[:, 512:1024], xh[:, 0, :]]
        tmp = route_buf[:, 1024:1536]
        nxT = [xhT[:, i, :, :] for i in range(2)]
        vr = route_buf[:, 1536:1664]
        er = route_buf[:, 1664:1760]
        sg = route_buf[:, 1760:1856]
        oh = [GW[:, 0, 128 * i:128 * i + 128].rearrange("p (k e) -> p k e", k=2) for i in range(2)]
        Mk = [GW[:, 1, 64 * i:64 * i + 64] for i in range(2)]
        C = GW[:, 1, 128:192]
        tb = GW[:, 1, 192:256]
        junk = GW[:, 1, 256:320]
        hsig = GW[:, 1, 320:352]
        slot = GW[:, 1, 352:352 + 2 * NB].bitcast(i32).rearrange("p (s k) -> p s k", k=2)
        weighted = GW[:, 1, 384:448]
        stack = [GW[:, 2, 128 * i:128 * i + 97] for i in range(2)]
        before = GW[:, 0, 256:384]
        stackT = [GW[0:97, 3, 128 * i:128 * i + 128] for i in range(2)]
        late = A[:, :]
        xg = [late[0:CAP, 512 * i:512 * i + 512] for i in range(XG)]
        o = 512 * XG
        ysb = [late[0:CAP, o + 512 * i:o + 512 * i + 512] for i in range(YS)]
        o += 512 * YS
        xe = [late[:, o + 320 * i:o + 320 * i + 320].rearrange("p (c t) -> p c t", c=DC) for i in range(2)]
        o += 640
        sl = [late[:, o + 160 * i:o + 160 * i + 160].rearrange("p (m t) -> p m t", m=HC) for i in range(2)]
        o += 320
        hT = [late[:, o + 160 * i:o + 160 * i + 160].rearrange("p (m t) -> p m t", m=HC) for i in range(2)]
        o += 320
        L = late[0:EXPERTS, o:o + CAP * REC]
        o += CAP * REC
        TOK = late[0:CAP, o:o + 64].bitcast(i32)
        DROW = late[0:CAP, o + 64:o + 128].bitcast(i32)
        CW = late[0:CAP, o + 128:o + 192]
        idx_g = late[0:CAP, o + 192:o + 192 + RING + AHEAD].bitcast(i32)
        idx_s = late[0:CAP, o + 208:o + 208 + RING].bitcast(i32)
        yfin = w13[:, 0:4, :, :, :].rearrange("p r a c h -> p (r a c h)").rearrange(
            "p (s k d) -> p s k d", s=NB, k=2)

        mv1 = small[:, 0:16].rearrange("p (s a) -> p s a", a=2)
        mv2 = small[:, 16:32].rearrange("p (s a) -> p s a", a=2)
        ve1, r1, nm1 = small[:, 32:40], small[:, 40:48], small[:, 48:56]
        ve2, r2, nm2, s2 = small[:, 56:64], small[:, 64:72], small[:, 72:80], small[:, 80:88]
        m8, i8 = small[:, 88:96], small[:, 96:104].bitcast(u32)
        idf = [small[:, 104 + 2 * i:106 + 2 * i] for i in range(2)]
        ssum, rsum = small[:, 108:109], small[:, 109:110]
        pos = small[:, 114:116]
        key8 = [small[:, 120 + 32 * i:128 + 32 * i] for i in range(2)]
        w8 = [small[:, 128 + 32 * i:136 + 32 * i] for i in range(2)]
        rec = small[:, 192:192 + NB * 2 * REC].rearrange("p (s k a) -> p s k a", k=2, a=REC)
        mn, mx, nwin = small[:, 136:137], small[:, 137:138], small[:, 138:139]
        spanf, spani = small[:, 139:140], small[:, 140:141].bitcast(i32)
        st6 = small[:, 142:148]
        rowz = GW[0:1, 0, 384:448]
        caps = rowz[0:1, 0:ROUNDS]
        over = rowz[0:1, 16:16 + ROUNDS]
        most, nround = rowz[0:1, 32:33], rowz[0:1, 33:34]
        stdv = ve2

        bank = [ctx.enter_context(nc.psum_tensor(f"bank{i}", [P, 512], f32)) for i in range(8)]

        edges_in, gw_in, raw_in, small_in, ws_in = (sem(s) for s in (
            "edges_in", "gw_in", "raw_in", "small_in", "ws_in"))
        x_in = [sem(f"x_in{i}") for i in range(4)]
        late_in = sem("late_in")
        consts = sem("consts")
        sentinel_out = sem("sentinel_out")
        dve_chain = sem("dve_chain")
        act_chain = sem("act_chain")
        pool_chain = sem("pool_chain")
        edge_prepped = sem("edge_prepped")
        edges_transposed = sem("edges_transposed")
        edges_ready = sem("edges_ready")
        rounds_ready = sem("rounds_ready")
        raw_transposed = sem("raw_transposed")
        raw_evac = sem("raw_evac")
        wsb_ready = sem("wsb_ready")
        sums_done = sem("sums_done")
        stats_ready = sem("stats_ready")
        std_ready = sem("std_ready")
        xh_ready = sem("xh_ready")
        xhT_ps = sem("xhT_ps")
        xhT_ready = sem("xhT_ready")
        hw_ps = sem("hw_ps")
        hw_ready = sem("hw_ready")
        key_copied, osl_chain, m_pool = sem("key_copied"), sem("osl_chain"), sem("m_pool")
        osl_ready = sem("osl_ready")
        m_ready = sem("m_ready")
        quad_done = [sem("first_quad_done"), sem("second_quad_done")]
        a_chain = sem("a_chain")
        win_chain = sem("win_chain")
        at_ps = sem("at_ps")
        at_act = sem("at_act")
        at_dve = sem("at_dve")
        out_ps = sem("out_ps")
        x1_ready = sem("x1_ready")
        mv1_ready, mv2_ready, r1_ready, r2_ready = (sem(s) for s in (
            "mv1_ready", "mv2_ready", "r1_ready", "r2_ready"))
        xt_ready, nx_ready = sem("xt_ready"), sem("nx_ready")
        nx_out = [sem(f"nx_out{i}") for i in range(2)]
        nxT_ps, nxT_ready = sem("nxT_ps"), sem("nxT_ready")
        route_ps, vr_ready, er_ready = sem("route_ps"), sem("vr_ready"), sem("er_ready")
        stack_ready, rank_ps, stackT_ready, rank_read = (sem(s) for s in (
            "stack_ready", "rank_ps", "stackT_ready", "rank_read"))
        z_ps, z_added = sem("z_ps"), sem("z_added")
        rec_ready = sem("rec_ready")
        rec_out = [sem(f"rec_out{i}") for i in range(2)]
        count_ready, count_ps = sem("count_ready"), sem("count_ps")
        tokens_ready = sem("tokens_ready")
        xg_clear = sem("xg_clear")
        w_in = [sem(f"w_in{i}") for i in range(RING)]
        list_in, list_ps, list_ready = sem("list_in"), sem("list_ps"), sem("list_ready")
        list_tok = sem("list_tok")
        idx_copied = sem("idx_copied")
        xg_in = [sem(f"xg_in{i}") for i in range(XG)]
        xe_ps, xe_ready, h_ps, sl_ready, hT_ready, y_ps, y_ready = (sem(s) for s in (
            "xe_ps", "xe_ready", "h_ps", "sl_ready", "hT_ready", "y_ps", "y_ready"))
        y_out = [sem(f"y_out{i}") for i in range(YS)]
        fin_in = [sem(f"fin_in{i}") for i in range(NB)]
        fin_ready = sem("fin_ready")
        out_done = sem("out_done")
        held = sem("held")

        def hold(engine):
            engine.sem_inc(held, 1)

        W1v = W1.rearrange("e (p c) h -> e p (c h)", c=DC)
        W3v = W3.rearrange("e (p c) h -> e p (c h)", c=DC)
        W2v = W2.rearrange("e (m p) d -> e p m d", p=P)
        block = ctx.enter_context(nc.Block())

        @block.sync
        def _(sp):
            edge_view = [a.rearrange("(t p) -> t p", p=P) for a in (dst, src, ew)]
            for to, a in zip((edge_dst, edge_src, edge_w), edge_view):
                sp.dma_start(to, a).then_inc(edges_in, 16)
            v3 = "e (c d) -> e c d"
            for to, a in ((raw_wg, Wg), (raw_g, gamma), (raw_b, beta)):
                sp.dma_start(to, a.rearrange(v3, c=4)).then_inc(raw_in, 16)
            sp.dma_start(raw_b13[:, 0:2, :], b1.rearrange(v3, c=HC)).then_inc(raw_in, 16)
            sp.dma_start(raw_b13[:, 2:4, :], b3.rearrange(v3, c=HC)).then_inc(raw_in, 16)
            sp.dma_start(gs4[:, 0, :], gs.rearrange("(p c) -> p c", c=DC)).then_inc(small_in, 16)
            sp.dma_start(gs4[:, 1, :], bs.rearrange("(p c) -> p c", c=DC)).then_inc(small_in, 16)
            sp.dma_start(bc[:, 0:64], bg.partition_broadcast(P)).then_inc(small_in, 16)
            sp.dma_start(bc[:, 64:96], bs1.partition_broadcast(P)).then_inc(small_in, 16)
            sp.dma_start(bc[:, 96:128], bs3.partition_broadcast(P)).then_inc(small_in, 16)
            sp.dma_start(Ws[:, :, 0:32], Ws1.rearrange("(p c) n -> p c n", c=DC)).then_inc(ws_in, 16)
            sp.dma_start(Ws[:, :, 32:64], Ws3.rearrange("(p c) n -> p c n", c=DC)).then_inc(ws_in, 16)
            xv = x.rearrange("(b p) d -> p b d", p=P)
            for i in range(4):
                sp.dma_start(X[:, 2 * i:2 * i + 2, :], xv[:, 2 * i:2 * i + 2, :]).then_inc(x_in[i], 16)
            sp.dma_start(GW[:, :, :], W.rearrange("(p c) n -> p c n", c=DC)).then_inc(gw_in, 16)
            sp.wait_ge(consts, 6)
            sp.dma_start(slots.rearrange("(p n) r -> p (n r)", p=P), sentinel).then_inc(sentinel_out, 16)

            def load_expert(e, u):
                sp.dma_start(w13[:, u, 0, :, :].rearrange("p c h -> p (c h)"), W1v[e]).then_inc(w_in[u], 16)
                sp.dma_start(w13[:, u, 1, :, :].rearrange("p c h -> p (c h)"), W3v[e]).then_inc(w_in[u], 16)
                sp.dma_start(w2[:, u, :, :], W2v[e]).then_inc(w_in[u], 16)

            for u in range(RING):
                load_expert(u, u)
            sp.wait_ge(edges_ready, 3)
            sp.dma_start(biasB, bias.partition_broadcast(P)).then_inc(late_in, 16)
            sp.dma_start(stackB[0:64, :], b2).then_inc(late_in, 16)
            sp.dma_start(stackB[64:96, :], Ws2).then_inc(late_in, 16)
            sp.dma_start(stackB[96:97, :], bs2.unsqueeze(0)).then_inc(late_in, 16)
            for s in range(NB):
                sp.wait_ge(nx_ready, s + 1)
                sp.dma_start(nx_rows[s * P:(s + 1) * P, :], nx[s % 2]).then_inc(nx_out[s % 2], 16)
            for i in range(2):
                sp.wait_ge(rec_out[i], 32 * NB // 2)
            sp.wait_ge(tokens_ready, 1)
            R2 = sp.value_load(rounds_sb[0:1, 1:2], min_val=1, max_val=ROUNDS)
            lists = slots.rearrange("(e n) r -> e (n r)", e=EXPERTS)
            with sp.Fori(0, R2) as r:
                sp.dma_start(L, lists[:, ds(r * (CAP * REC), CAP * REC)]).then_inc(list_in, 16)
                with sp.Fori(0, GROUPS - 1) as g:
                    for u in range(RING):
                        used = sp.snap(r * EXPERTS + g * RING + (u + 1))
                        e = sp.snap(g * RING + (RING + u))
                        sp.wait_ge(y_ps, used)
                        w = W1.rearrange("e (p c) h -> e p (c h)", c=DC)
                        load_expert(e, u)
                with sp.If(r + 1 < R2):
                    for u in range(RING):
                        used = sp.snap(r * EXPERTS + (EXPERTS - RING + u + 1))
                        sp.wait_ge(y_ps, used)
                        load_expert(u, u)
            last = sp.snap(R2 * (16 * EXPERTS // YS))
            yv = y_rows.rearrange("(k s p) d -> s p k d", k=2, p=P)
            for i in range(YS):
                sp.wait_ge(y_out[i], last)
            for s in range(NB):
                sp.dma_start(yfin[:, s, :, :], yv[s]).then_inc(fin_in[s], 16)
            for s in range(NB):
                sp.wait_ge(fin_ready, s + 1)
                sp.dma_start(out[s * P:(s + 1) * P, :], X[:, s, :]).then_inc(out_done, 16)
            sp.wait_ge(out_done, 16 * NB)

        @block.gpsimd
        def _(pool):
            g = nc.gpsimd
            g.memset(ones[:, :], 1.0).then_inc(consts, 1)
            pool.wait_ge(consts, 1)
            g.affine_select(out=ident[:, :], in_=ones[:, :], pattern=[[-1, P]], compare_op=ALU.is_equal,
                            fill=0.0, base=0, channel_multiplier=1).then_inc(consts, 1)
            g.iota(iota[:, :], pattern=[[1, P]], base=0, channel_multiplier=0,
                   allow_small_or_imprecise_dtypes=True).then_inc(consts, 1)
            g.iota(tokcol[:, :], pattern=[[1, 1]], base=0, channel_multiplier=1,
                   allow_small_or_imprecise_dtypes=True).then_inc(consts, 1)
            g.memset(mhalf[:, :], -0.5).then_inc(consts, 1)
            g.memset(sentinel, NOWHERE).then_inc(consts, 1)
            g.memset(rec, 0.0).then_inc(consts, 1)
            pool.wait_ge(consts, 7)
            g.iota(rec[:, :, :, 0], pattern=[[P, NB], [0, 2]], base=0, channel_multiplier=1,
                   allow_small_or_imprecise_dtypes=True).then_inc(consts, 1)
            g.iota(rec[:, :, :, 1], pattern=[[P, NB], [N, 2]], base=0, channel_multiplier=1,
                   allow_small_or_imprecise_dtypes=True).then_inc(consts, 1)
            pool.wait_ge(small_in, 80)
            pool.wait_ge(ws_in, 32)
            for c in range(DC):
                g.tensor_scalar(R[:, c, 64:128], Ws[:, c, :], gs4[:, 0, c:c + 1], None, ALU.mult)
                ins = g.tensor_scalar(Wsb[:, c, :], Ws[:, c, :], gs4[:, 1, c:c + 1], None, ALU.mult)
            ins.then_inc(wsb_ready, 1)
            pool.wait_ge(edges_ready, 1)
            R1 = pool.value_load(rounds_sb[0:1, 0:1], min_val=1, max_val=N // WIN)

            def pair(r, j, first):
                half = (r * (NB // 2) + j) * 4
                for h in range(4):
                    if not first or h >= 2:
                        pool.wait_ge(m_pool, (half + (h - 1)) * 2)
                        hold(pool)
                    g.tensor_copy(key8[h % 2], eT[:, 0, ds(j * 32 + 8 * h, 8)]).then_inc(key_copied, 1)
                    g.tensor_copy(w8[h % 2], eT[:, 2, ds(j * 32 + 8 * h, 8)]).then_inc(key_copied, 1)
                    pool.wait_ge(key_copied, (half + (h + 1)) * 2)
                    for q in (2 * h, 2 * h + 1):
                        if not first or q >= 2:
                            pool.wait_ge(quad_done[q % 2], half + q // 2)
                        hold(pool)
                        for k in range(QUAD - 1):
                            t = (q % 2) * QUAD + k
                            ins = g.tensor_scalar(M[:, q % 2, k, :], iota[:, :], key8[h % 2][:, t:t + 1], w8[h % 2][:, t:t + 1],
                                                  ALU.is_equal, ALU.mult)
                        ins.then_inc(m_pool, 1)

            pair(0, 0, True)
            with pool.Fori(1, NB // 2) as j:
                pair(0, j, False)
            with pool.If(R1 > 1):
                with pool.Fori(1, R1) as r:
                    pool.wait_ge(win_chain, r * 3)
                    hold(pool)
                    with pool.Fori(0, NB // 2) as j:
                        pair(r, j, False)
            pool_n = [0]

            def link(ins):
                pool_n[0] += 1
                ins.then_inc(pool_chain, 1)
                pool.wait_ge(pool_chain, pool_n[0])

            def scatter_records(s):
                pool.wait_ge(rec_ready, s + 1)
                if s == 0:
                    pool.wait_ge(sentinel_out, 16)
                for k in range(2):
                    g.indirect_dma_start(slots, bass.IndirectOffsetOnAxis(ap=slot[:, s, k:k + 1], axis=0),
                                         rec[:, s, k, :], None).then_inc(rec_out[s % 2], 16)

            pool.wait_ge(edges_ready, 3)
            link(g.affine_select(out=before, in_=ones[:, :], pattern=[[1, P]], compare_op=ALU.is_gt,
                                 fill=0.0, base=0, channel_multiplier=-1))
            for s in range(NB + 2):
                if s < NB:
                    pool.wait_ge(mv1_ready, s + 1)
                    c = slice(s, s + 1)
                    link(g.tensor_scalar(ve1[:, c], mv1[:, s, 1:2], EPS, None, ALU.add))
                    link(g.tensor_tensor(r1[:, c], ve1[:, c], mhalf[:, :], ALU.pow))
                    link(g.tensor_tensor(nm1[:, c], mv1[:, s, 0:1], r1[:, c], ALU.mult))
                    g.tensor_scalar(nm1[:, c], nm1[:, c], -1.0, None, ALU.mult).then_inc(r1_ready, 1)
                if s >= 2:
                    scatter_records(s - 2)
                if s < NB:
                    pool.wait_ge(mv2_ready, s + 1)
                    link(g.tensor_scalar(ve2[:, c], mv2[:, s, 1:2], EPS, None, ALU.add))
                    link(g.tensor_tensor(r2[:, c], ve2[:, c], mhalf[:, :], ALU.pow))
                    link(g.tensor_tensor(s2[:, c], ve2[:, c], r2[:, c], ALU.mult))
                    link(g.tensor_tensor(nm2[:, c], mv2[:, s, 0:1], r2[:, c], ALU.mult))
                    g.tensor_scalar(nm2[:, c], nm2[:, c], -1.0, None, ALU.mult).then_inc(r2_ready, 1)
            pool.wait_ge(at_ps, 2 * NB)
            g.memset(late[0:CAP, 0:512 * XG], 0.0).then_inc(xg_clear, 1)
            pool.wait_ge(xg_clear, 1)
            pool.wait_ge(nx_out[0], 16 * NB // 2)
            pool.wait_ge(nx_out[1], 16 * NB // 2)
            pool.wait_ge(tokens_ready, 1)
            R2 = pool.value_load(rounds_sb[0:1, 1:2], min_val=1, max_val=ROUNDS)

            def gather(col, b):
                g.indirect_dma_start(xg[b], None, nx_rows, bass.IndirectOffsetOnAxis(ap=idx_g[:, col:col + 1], axis=0),
                                     bounds_check=N - 1, oob_is_err=False).then_inc(xg_in[b], 16)

            def scatter(u, count):
                pool.wait_ge(y_ready, count)
                hold(pool)
                g.indirect_dma_start(y_rows, bass.IndirectOffsetOnAxis(ap=idx_s[:, u:u + 1], axis=0), ysb[u % YS], None,
                                     bounds_check=2 * N - 1, oob_is_err=False).then_inc(y_out[u % YS], 16)

            with pool.Fori(0, R2) as r:
                pool.wait_ge(list_ready, r + 1)
                hold(pool)
                g.tensor_copy(idx_g[:, 0:AHEAD], TOK[:, 0:AHEAD]).then_inc(idx_copied, 1)
                pool.wait_ge(idx_copied, r * (2 * GROUPS + 1) + 1)
                hold(pool)
                for u in range(AHEAD):
                    gather(u, u)

                def group(gi, first, last):
                    n = RING if last else RING + AHEAD
                    base = r * EXPERTS + gi * RING
                    for b in range(AHEAD):
                        pool.wait_ge(xg_in[b], (r * GROUPS + gi + 1) * 16)
                    hold(pool)
                    g.tensor_copy(idx_g[:, 0:n], TOK[:, ds(gi * RING, n)]).then_inc(idx_copied, 1)
                    if not first:
                        for b in range(YS):
                            pool.wait_ge(y_out[b], (r * (EXPERTS // YS) + gi * (RING // YS)) * 16)
                        hold(pool)
                    g.tensor_copy(idx_s[:, :], DROW[:, ds(gi * RING, RING)]).then_inc(idx_copied, 1)
                    pool.wait_ge(idx_copied, r * (2 * GROUPS + 1) + gi * 2 + 3)
                    hold(pool)
                    for u in range(RING):
                        if not (last and u >= RING - AHEAD):
                            if not first or u + AHEAD >= XG:
                                pool.wait_ge(xe_ps, base + (u + AHEAD - XG + 1))
                                hold(pool)
                            gather(u + AHEAD, (u + AHEAD) % XG)
                        if u:
                            scatter(u - 1, base + u)
                    scatter(RING - 1, base + RING)

                group(0, True, False)
                with pool.Fori(1, GROUPS - 1) as gi:
                    group(gi, False, False)
                group(GROUPS - 1, False, True)
                for b in range(YS):
                    pool.wait_ge(y_out[b], (r + 1) * (16 * EXPERTS // YS))

        @block.scalar
        def _(act):
            a = nc.scalar
            a.memzero(A[:, :]).then_inc(a_chain, 1)
            act.wait_ge(raw_transposed, 1)
            a.copy(R[:, :, 0:64], bank[2][:, 0:256].rearrange("p (c e) -> p c e", c=DC)).then_inc(raw_evac, 1)
            a.copy(gT[:, :, :].rearrange("p c e -> p (c e)"), bank[2][:, 256:512]).then_inc(raw_evac, 1)
            act.wait_ge(raw_transposed, 2)
            a.copy(bT[:, :, :].rearrange("p c e -> p (c e)"), bank[3][:, 0:256]).then_inc(raw_evac, 1)
            a.copy(b13T[:, :, :, :].rearrange("p a m e -> p (a m e)"), bank[3][:, 256:512]).then_inc(raw_evac, 1)
            act.wait_ge(stats_ready, 1)
            a.activation(stdv, mv[:, :, 1], ACT.Sqrt, bias=eps_c[:, :]).then_inc(std_ready, 1)
            act.wait_ge(edges_ready, 1)
            R1 = act.value_load(rounds_sb[0:1, 0:1], min_val=1, max_val=N // WIN)
            act.wait_ge(sentinel_out, 16)
            act.wait_ge(sums_done, 1)

            def one_hots(half, j, h, first):
                if not first or h >= 2:
                    act.wait_ge(quad_done[1], half + (h - 1))
                for k in range(8):
                    ins = a.activation(osl[:, h % 2, k, :], iota[:, :], ACT.Abs, bias=eT[:, 1, ds(j * 32 + 8 * h + k, 1)])
                ins.then_inc(osl_chain, 1)
                act.wait_ge(osl_chain, half + (h + 1))
                a.activation(osl[:, h % 2, :, :], osl[:, h % 2, :, :], ACT.Relu, scale=-1.0, bias=1.0).then_inc(osl_ready, 1)

            def x_transposed(g, u):
                act.wait_ge(xhT_ps, g + 1)
                a.copy(xhT[:, u, :, :].rearrange("p c n -> p (c n)"), bank[4 + u][:, :]).then_inc(xhT_ready, 1)

            def x_times_w(g, u):
                act.wait_ge(hw_ps, g + 1)
                a.copy(HW[:, ds(g, 1), :].rearrange("p a n -> p (a n)"), bank[6 + u][:, :]).then_inc(hw_ready, 1)

            def pair(j, first):
                half = j * 4
                one_hots(half, j, 0, first)
                if not first:
                    x_times_w(j * 2 - 1, 1)
                x_transposed(j * 2, 0)
                one_hots(half, j, 1, first)
                one_hots(half, j, 2, first)
                x_times_w(j * 2, 0)
                x_transposed(j * 2 + 1, 1)
                one_hots(half, j, 3, first)

            pair(0, True)
            with act.Fori(1, NB // 2) as j:
                pair(j, False)
            x_times_w(NB - 1, 1)
            with act.If(R1 > 1):
                with act.Fori(1, R1) as r:
                    with act.Fori(0, NB // 2) as j:
                        for h in range(4):
                            one_hots((r * (NB // 2) + j) * 4, j, h, False)

            def at_half(s):
                act.wait_ge(at_ps, 2 * s + 1)
                a.copy(AT[:, s % 2, 0:4, :].rearrange("p k n -> p (k n)"), bank[2 * (s % 2)][:, :]).then_inc(at_act, 1)

            at_half(0)
            for s in range(NB + 2):
                if s + 1 < NB:
                    if s >= 1:
                        act.wait_ge(out_ps, s)
                    at_half(s + 1)
                if s >= 2:
                    t = s - 2
                    act.wait_ge(vr_ready, t + 1)
                    a.activation(er, er, ACT.Exp, scale=-1.0).then_inc(er_ready, 1)
                if 1 <= s <= NB:
                    t = s - 1
                    act.wait_ge(nxT_ps, t + 1)
                    a.copy(nxT[t % 2].rearrange("p c n -> p (c n)"), bank[6][:, :]).then_inc(nxT_ready, 1)
                if s < NB:
                    act.wait_ge(r1_ready, s + 1)
                    a.activation(xt, X[:, s, :], ACT.Identity, scale=r1[:, s:s + 1], bias=nm1[:, s:s + 1]).then_inc(xt_ready, 1)
                    act.wait_ge(xt_ready, s + 1)
                    act.wait_ge(r2_ready, s + 1)
                    if s >= 2:
                        act.wait_ge(nx_out[s % 2], 16 * (s // 2))
                        act.wait_ge(nxT_ps, s - 1)
                    a.activation(nx[s % 2], xt, ACT.Identity, scale=r2[:, s:s + 1], bias=nm2[:, s:s + 1]).then_inc(nx_ready, 1)
            act.wait_ge(tokens_ready, 1)
            R2 = act.value_load(rounds_sb[0:1, 1:2], min_val=1, max_val=ROUNDS)
            with act.Fori(0, R2) as r:
                def group(g, first):
                    base = r * EXPERTS + g * RING

                    def silu(u):
                        act.wait_ge(h_ps, base + u + 1)
                        for m in range(HC):
                            ins = a.activation(sl[u % 2][:, m, :], bank[2 + u % 2][:, m * CAP:(m + 1) * CAP], ACT.Silu,
                                               bias=b13T[:, 0, m, ds(g * RING + u, 1)])
                        ins.then_inc(sl_ready, 1)

                    def result(u):
                        act.wait_ge(y_ps, base + u + 1)
                        if not first or u >= YS:
                            act.wait_ge(y_out[u % YS], (r * (EXPERTS // YS) + g * (RING // YS) + u // YS) * 16)
                        a.activation(ysb[u % YS], bank[6 + u % 2][0:CAP, :], ACT.Copy,
                                     scale=CW[:, ds(g * RING + u, 1)]).then_inc(y_ready, 1)

                    for u in range(RING):
                        silu(u)
                        if u:
                            result(u - 1)
                    result(RING - 1)

                act.wait_ge(list_ready, r + 1)
                group(0, True)
                with act.Fori(1, GROUPS) as g:
                    group(g, False)

        @block.vector
        def _(dve):
            v = nc.vector
            chain = [0]

            def link(ins):
                chain[0] += 1
                ins.then_inc(dve_chain, 1)
                dve.wait_ge(dve_chain, chain[0])

            def mark(ins):
                chain[0] += 1
                ins.then_inc(dve_chain, 1)
                return chain[0]

            def need(*marks):
                dve.wait_ge(dve_chain, max(marks))

            link(v.memset(eps_c[:, :], EPS))
            dve.wait_ge(edges_in, 48)
            c_d8 = mark(v.tensor_scalar(d8, edge_dst, 3, None, ALU.arith_shift_left))
            c_hi = mark(v.tensor_scalar(shi, edge_src, 7, None, ALU.arith_shift_right))
            c_lo = mark(v.tensor_scalar(slo, edge_src, P - 1, None, ALU.bitwise_and))
            need(c_d8)
            mark(v.tensor_reduce(mn, d8, AX, ALU.min))
            c_mx = mark(v.tensor_reduce(mx, d8, AX, ALU.max))
            need(c_hi)
            c_key = mark(v.tensor_tensor(key, d8, shi, ALU.add))
            need(c_lo, c_mx)
            mark(v.tensor_scalar(slof, slo, -1.0, None, ALU.mult))
            c_sp = mark(v.tensor_tensor(spani, mx, mn, ALU.subtract))
            need(c_key)
            mark(v.tensor_scalar(key, key, mn, None, ALU.subtract))
            need(c_sp)
            link(v.tensor_scalar(spani, spani, 7, None, ALU.arith_shift_right))
            v.tensor_scalar(nwin, spani, 1.0, None, ALU.add).then_inc(edge_prepped, 1)
            dve.wait_ge(edges_transposed, 1)
            link(v.tensor_copy(eT[:, :, :].rearrange("p a t -> p (a t)"), bank[0][:, 0:3 * P]))
            link(v.tensor_copy(wrow[:, :], bank[1][0:1, 0:2 * P]))
            link(v.tensor_reduce(rounds_sb[0:1, 0:1], wrow[:, P:2 * P], AX, ALU.max))
            v.tensor_copy(wbase, wrow[:, 0:P]).then_inc(edges_ready, 1)
            for b in range(NB):
                if b % 2 == 0:
                    dve.wait_ge(x_in[b // 2], 16)
                c_st = mark(v.bn_stats(stats[:, 6 * b:6 * b + 6], X[:, b, :]))
            need(c_st)
            for b in range(NB):
                ins = v.bn_aggr(mv[:, b, :], stats[:, 6 * b:6 * b + 6])
            ins.then_inc(stats_ready, 1)
            dve.wait_ge(std_ready, 1)
            link(v.reciprocal(rstd[:, :], stdv))
            dve.wait_ge(edges_ready, 1)
            R1 = dve.value_load(rounds_sb[0:1, 0:1], min_val=1, max_val=N // WIN)

            def sum_pair(r, j, with_x):
                if with_x:
                    for u in range(2):
                        b = j * 2 + u
                        v.tensor_scalar(xh[:, u, :], X[:, ds(b, 1), :].rearrange("p a n -> p (a n)"),
                                        mv[:, ds(b, 1), 0], rstd[:, ds(b, 1)],
                                        ALU.subtract, ALU.mult).then_inc(xh_ready, 1)
                done = dve.snap((r * (NB // 2) + j) * 4)
                added = dve.snap(done * (2 * QUAD))

                def bases(q):
                    _, at = nc.values_load_multi_w_load_instructions(
                        wbase[0:1, ds(j * 32 + QUAD * q, QUAD)], engines=[mybir.EngineType.DVE],
                        min_val=0, max_val=8 * N, skip_runtime_bounds_check_because="DVE bounded them by min and the keys are >= 0")
                    return at

                def sums(q, at):
                    dve.wait_ge(quad_done[q % 2], done + (q // 2 + 1))
                    for k in range(QUAD):
                        to = A[:, ds(at[k], P)]
                        dve.wait_ge(a_chain, added + (QUAD * q + k + 1))
                        v.tensor_tensor(to, to, bank[2 + q % 2][:, k * P:(k + 1) * P], ALU.add).then_inc(a_chain, 1)

                for q in range(8):
                    t, k = j * 32 + (QUAD * q + QUAD - 1), QUAD - 1
                    v.tensor_scalar(M[:, q % 2, k, :], iota[:, :], eT[:, 0, ds(t, 1)], eT[:, 2, ds(t, 1)],
                                    ALU.is_equal, ALU.mult).then_inc(m_ready, 1)
                    if q:
                        sums(q - 1, at)
                    at = bases(q)
                sums(7, at)

            with dve.Fori(0, NB // 2) as j:
                sum_pair(0, j, True)
            more = dve.snap(R1)
            with dve.If(more > 1):
                with dve.Fori(1, R1) as r:
                    w = dve.snap(r * 3)
                    v.tensor_scalar(eT[:, 0, :], eT[:, 0, :], float(P), None, ALU.subtract).then_inc(win_chain, 1)
                    v.tensor_scalar(wrow[:, 0:P], wrow[:, 0:P], float(P), None, ALU.add).then_inc(win_chain, 1)
                    dve.wait_ge(win_chain, w - 1)
                    v.tensor_scalar(wbase, wrow[:, 0:P], float(8 * N), None, ALU.min).then_inc(win_chain, 1)
                    dve.wait_ge(win_chain, w)
                    hold(dve)
                    with dve.Fori(0, NB // 2) as j:
                        sum_pair(r, j, False)
            dve.wait_ge(a_chain, R1 * TILES + 1)
            dve.wait_ge(hw_ps, NB)
            dve.wait_ge(sums_done, 1)
            link(v.tensor_copy(rowWg[:, :], bank[1][:, 256:320]))
            link(v.tensor_tensor(bc[:, 64:128], bc[:, 64:128], bank[1][:, 320:384], ALU.add))
            v.memset(C, 0.0).then_inc(edges_ready, 1)
            dve.wait_ge(edges_ready, 2)
            for i in range(2):
                ins = v.memset(stack[i][:, 96:97], 1.0)
            ins.then_inc(edges_ready, 1)

            def at_half(s):
                dve.wait_ge(at_ps, 2 * s + 2)
                v.tensor_copy(AT[:, s % 2, 4:8, :].rearrange("p k n -> p (k n)"), bank[2 * (s % 2) + 1][:, :]).then_inc(at_dve, 1)

            def relu_add(s):
                dve.wait_ge(out_ps, s + 1)
                if s == 0:
                    dve.wait_ge(late_in, 64)
                link(v.tensor_tensor(tmp, bank[4 + s % 2][:, :], biasB, ALU.add))
                v.scalar_tensor_tensor(X[:, s, :], tmp, 0.0, X[:, s, :], ALU.max, ALU.add).then_inc(x1_ready, 1)
                dve.wait_ge(x1_ready, s + 1)
                link(v.bn_stats(st6, X[:, s, :]))
                v.bn_aggr(mv1[:, s, :], st6).then_inc(mv1_ready, 1)

            def route(t):
                i = t % 2
                cw = rec[:, t, :, 2]
                dve.wait_ge(route_ps, t + 1)
                c_tb = mark(v.scalar_tensor_tensor(tb, rowWg[:, :], mv2[:, t, 0:1], bc[:, 0:64], ALU.mult, ALU.add))
                mark(v.tensor_tensor(vr[:, 64:128], bank[7][:, 64:128], bc[:, 64:128], ALU.add))
                need(c_tb)
                link(v.scalar_tensor_tensor(vr[:, 0:64], bank[7][:, 0:64], s2[:, t:t + 1], tb, ALU.mult, ALU.add))
                v.tensor_scalar(er, vr[:, 0:96], -87.0, None, ALU.max).then_inc(vr_ready, 1)
                if t >= 1:
                    add_shared(t - 1)
                dve.wait_ge(er_ready, t + 1)
                link(v.tensor_scalar(er, er, 1.0, None, ALU.add))
                link(v.reciprocal(sg, er))
                c_m8 = mark(v.max(m8, sg[:, 0:64]))
                c_hs = mark(v.tensor_tensor(hsig, vr[:, 64:96], sg[:, 64:96], ALU.mult))
                need(c_m8)
                c_i8 = mark(v.max_index(i8, m8, sg[:, 0:64]))
                c_ss = mark(v.tensor_tensor(ssum, m8[:, 0:1], m8[:, 1:2], ALU.add))
                need(c_hs, c_i8)
                c_id = mark(v.tensor_copy(idf[i], i8[:, 0:2]))
                mark(v.tensor_tensor(stack[i][:, 64:96], hsig, vr[:, 96:128], ALU.mult))
                need(c_ss, c_id)
                c_rs = mark(v.reciprocal(rsum, ssum))
                c_oh = mark(v.tensor_tensor(oh[i], iota[:, 0:64].unsqueeze(1).broadcast_to([P, 2, 64]),
                                            idf[i].unsqueeze(2).broadcast_to([P, 2, 64]), ALU.is_equal))
                need(c_rs)
                c_cw = mark(v.tensor_scalar(cw, m8[:, 0:2], rsum, None, ALU.mult))
                need(c_oh)
                mark(v.tensor_tensor(Mk[i], oh[i][:, 0, :], oh[i][:, 1, :], ALU.add))
                need(c_cw)
                link(v.tensor_scalar(weighted, oh[i][:, 0, :], rec[:, t, 0, 2:3], None, ALU.mult))
                v.scalar_tensor_tensor(stack[i][:, 0:64], oh[i][:, 1, :], rec[:, t, 1, 2:3], weighted,
                                       ALU.mult, ALU.add).then_inc(stack_ready, 1)

            def rank(t):
                i = t % 2
                dve.wait_ge(rank_ps, t + 1)
                v.tensor_copy(stackT[i], bank[7][0:97, 0:P]).then_inc(stackT_ready, 1)
                for k in range(2):
                    c_pos = mark(v.tensor_tensor_reduce(out=junk if k else tb, in0=oh[i][:, k, :], in1=bank[7][:, 128:192],
                                                        scale=1.0, scalar=0.0, op0=ALU.mult, op1=ALU.add,
                                                        accum_out=pos[:, k:k + 1]))
                mark(v.tensor_tensor(C, C, Mk[i], ALU.add))
                need(c_pos)
                v.scalar_tensor_tensor(slot[:, t, :], idf[i], float(LIST), pos, ALU.mult, ALU.add).then_inc(rec_ready, 1)

            def add_shared(t):
                dve.wait_ge(z_ps, t + 1)
                v.tensor_tensor(X[:, t, :], X[:, t, :], bank[6][:, :], ALU.add).then_inc(z_added, 1)

            at_half(0)
            for s in range(NB + 3):
                if s + 1 < NB:
                    if s >= 1:
                        dve.wait_ge(out_ps, s)
                    at_half(s + 1)
                if 2 <= s < NB + 2:
                    route(s - 2)
                if s < NB:
                    relu_add(s)
                if 2 <= s < NB + 2:
                    rank(s - 2)
                    if s == NB + 1:
                        link(v.tensor_scalar(caps, iota[0:1, 0:ROUNDS], float(CAP), None, ALU.mult))
                        dve.wait_ge(count_ps, 1)
                        link(v.tensor_reduce(most, bank[5][0:1, 0:64], AX, ALU.max))
                        link(v.tensor_scalar(over, caps, most, None, ALU.is_lt))
                        link(v.tensor_reduce(nround, over, AX, ALU.add))
                        v.tensor_copy(rounds_sb[0:1, 1:2], nround).then_inc(tokens_ready, 1)
                if s < NB:
                    dve.wait_ge(xt_ready, s + 1)
                    link(v.bn_stats(st6, xt))
                    v.bn_aggr(mv2[:, s, :], st6).then_inc(mv2_ready, 1)
            add_shared(NB - 1)
            dve.wait_ge(tokens_ready, 1)
            R2 = dve.value_load(rounds_sb[0:1, 1:2], min_val=1, max_val=ROUNDS)
            with dve.Fori(0, R2) as r:
                dve.wait_ge(list_ps, r + 1)
                v.tensor_copy(TOK, bank[6][0:CAP, 0:64])
                v.tensor_copy(DROW, bank[6][0:CAP, 64:128])
                v.tensor_copy(CW, bank[6][0:CAP, 128:192]).then_inc(list_ready, 1)

                def rows(gi, u, count):
                    dve.wait_ge(xe_ps, count)
                    b = u % 2
                    for c in range(DC):
                        e = gi * RING + u
                        ins = v.tensor_scalar(xe[b][:, c, :], bank[b][:, c * CAP:(c + 1) * CAP], gT[:, c, ds(e, 1)],
                                              bT[:, c, ds(e, 1)], ALU.mult, ALU.add)
                    ins.then_inc(xe_ready, 1)

                rows(0, 0, r * EXPERTS + 1)

                def group(gi, last):
                    base = r * EXPERTS + gi * RING
                    for u in range(RING):
                        if not (last and u == RING - 1):
                            rows(gi, u + 1, base + u + 2)
                        dve.wait_ge(sl_ready, base + u + 1)
                        for m in range(HC):
                            ins = v.scalar_tensor_tensor(hT[u % 2][:, m, :], bank[4 + u % 2][:, m * CAP:(m + 1) * CAP],
                                                         b13T[:, 1, m, ds(gi * RING + u, 1)], sl[u % 2][:, m, :],
                                                         ALU.add, ALU.mult)
                        ins.then_inc(hT_ready, 1)

                with dve.Fori(0, GROUPS - 1) as gi:
                    group(gi, False)
                group(GROUPS - 1, True)
                for i in range(YS):
                    dve.wait_ge(y_out[i], (r + 1) * (16 * EXPERTS // YS))
            for s in range(NB):
                dve.wait_ge(fin_in[s], 16)
                link(v.tensor_tensor(X[:, s, :], X[:, s, :], yfin[:, s, 0, :], ALU.add))
                v.tensor_tensor(X[:, s, :], X[:, s, :], yfin[:, s, 1, :], ALU.add).then_inc(fin_ready, 1)

        @block.tensor
        def _(pe):
            t = nc.tensor
            pe.wait_ge(consts, 5)
            pe.wait_ge(edge_prepped, 1)
            t.transpose(bank[0][:, 0:P], key, ident[:, :])
            t.transpose(bank[0][:, P:2 * P], slof, ident[:, :])
            t.transpose(bank[0][:, 2 * P:3 * P], edge_w, ident[:, :])
            t.matmul(bank[1][0:1, 0:P], mn, ident[:, :], start=True, stop=True)
            t.matmul(bank[1][0:1, P:2 * P], nwin, ident[:, :], start=True, stop=True).then_inc(edges_transposed, 1)
            pe.wait_ge(raw_in, 80)
            id64 = ident[0:64, 0:64]
            for i, raw in enumerate((raw_wg, raw_g, raw_b)):
                flat = raw.rearrange("e c d -> e (c d)")
                for c in range(DC):
                    ins = t.transpose(bank[2 + i // 2][:, (i % 2) * 256 + 64 * c:(i % 2) * 256 + 64 * c + 64],
                                      flat[:, c:c + DC * (P - 1) + 1:DC], id64)
                if i == 1:
                    ins.then_inc(raw_transposed, 1)
            for c in range(2 * HC):
                ins = t.transpose(bank[3][:, 256 + 64 * c:320 + 64 * c], raw_b13[:, c, :], id64)
            ins.then_inc(raw_transposed, 1)
            pe.wait_ge(raw_evac, 4)
            pe.wait_ge(wsb_ready, 1)
            pe.wait_ge(edges_ready, 1)
            for c in range(DC):
                t.matmul(bank[1][:, 256:320], ones[:, :], R[:, c, 0:64], start=(c == 0), stop=(c == DC - 1))
            for c in range(DC):
                ins = t.matmul(bank[1][:, 320:384], ones[:, :], Wsb[:, c, :], start=(c == 0), stop=(c == DC - 1))
            ins.then_inc(sums_done, 1)
            pe.wait_ge(edges_ready, 1)
            R1 = pe.value_load(rounds_sb[0:1, 0:1], min_val=1, max_val=N // WIN)
            pe.wait_ge(gw_in, 16)

            def pair(r, j, with_x):
                half = pe.snap((r * (NB // 2) + j) * 4)
                quad = pe.snap(half * 2)
                for u in range(2):
                    if with_x:
                        pe.wait_ge(xh_ready, j * 2 + u + 1)
                        for c in range(DC):
                            ins = t.transpose(bank[4 + u][:, c * P:(c + 1) * P], xh[:, u, c:c + DC * (P - 1) + 1:DC], ident[:, :])
                        ins.then_inc(xhT_ps, 1)
                    for q in range(4 * u, 4 * u + 4):
                        if q % 2 == 0:
                            pe.wait_ge(osl_ready, half + (q // 2 + 1))
                        pe.wait_ge(m_pool, quad + (q + 1))
                        pe.wait_ge(m_ready, quad + (q + 1))
                        for k in range(QUAD):
                            ins = t.matmul(bank[2 + q % 2][:, k * P:(k + 1) * P], osl[:, (q // 2) % 2, (q % 2) * QUAD + k, :],
                                           M[:, q % 2, k, :], start=True, stop=True)
                        ins.then_inc(quad_done[q % 2], 1)
                    if with_x:
                        pe.wait_ge(xhT_ready, j * 2 + u + 1)
                        for c in range(DC):
                            ins = t.matmul(bank[6 + u][:, :], xhT[:, u, c, :], GW[:, c, :], start=(c == 0), stop=(c == DC - 1))
                        ins.then_inc(hw_ps, 1)

            with pe.Fori(0, NB // 2) as j:
                pair(0, j, True)
            with pe.If(R1 > 1):
                with pe.Fori(1, R1) as r:
                    with pe.Fori(0, NB // 2) as j:
                        pair(r, j, False)
            pe.wait_ge(edges_ready, 3)
            pe.wait_ge(hw_ready, NB)
            A3 = A[:, :].rearrange("p (n s) -> p n s", s=8)

            def transpose_a(s):
                for k in range(NB):
                    ins = t.transpose(bank[2 * (s % 2) + k // 4][:, (k % 4) * P:(k % 4 + 1) * P], A3[:, k * P:(k + 1) * P, s], ident[:, :])
                    if k % 4 == 3:
                        ins.then_inc(at_ps, 1)

            def sum_messages(s, ks):
                if ks[0] == 0:
                    pe.wait_ge(at_act, s + 1)
                    pe.wait_ge(at_dve, s + 1)
                    if s >= 2:
                        pe.wait_ge(x1_ready, s - 1)
                for k in ks:
                    ins = t.matmul(bank[4 + s % 2][:, :], AT[:, s % 2, k, :], HW[:, k, :], start=(k == 0), stop=(k == NB - 1))
                if ks[-1] == NB - 1:
                    ins.then_inc(out_ps, 1)

            def transpose_nx(b):
                pe.wait_ge(nx_ready, b + 1)
                if b >= 2:
                    pe.wait_ge(z_added, b - 1)
                for c in range(DC):
                    ins = t.transpose(bank[6][:, c * P:(c + 1) * P], nx[b % 2][:, c:c + DC * (P - 1) + 1:DC], ident[:, :])
                ins.then_inc(nxT_ps, 1)

            def route(b):
                pe.wait_ge(nxT_ready, b + 1)
                if b >= 1:
                    pe.wait_ge(rec_ready, b)
                for c in range(DC):
                    ins = t.matmul(bank[7][:, 0:P], nxT[b % 2][:, c, :], R[:, c, :], start=(c == 0), stop=(c == DC - 1))
                ins.then_inc(route_ps, 1)

            def rank(b):
                pe.wait_ge(stack_ready, b + 1)
                t.transpose(bank[7][0:97, 0:P], stack[b % 2], ident[:, :])
                t.matmul(bank[7][:, 128:192], before, Mk[b % 2], start=True, stop=False)
                if b >= 1:
                    pe.wait_ge(rec_ready, b)
                t.matmul(bank[7][:, 128:192], ones[:, :], C, start=False, stop=True).then_inc(rank_ps, 1)

            def shared(b):
                pe.wait_ge(stackT_ready, b + 1)
                pe.wait_ge(nxT_ready, min(b + 2, NB))
                t.matmul(bank[6][:, :], stackT[b % 2], stackB, start=True, stop=True).then_inc(z_ps, 1)

            transpose_a(0)
            for s in range(NB + 3):
                if s + 1 < NB:
                    transpose_a(s + 1)
                if s < NB:
                    sum_messages(s, range(0, 4))
                if s >= 3:
                    shared(s - 3)
                if 2 <= s < NB + 2:
                    route(s - 2)
                if s < NB:
                    sum_messages(s, range(4, 8))
                if 1 <= s <= NB:
                    transpose_nx(s - 1)
                if 2 <= s < NB + 2:
                    rank(s - 2)
                    if s == NB + 1:
                        pe.wait_ge(rec_ready, NB)
                        t.matmul(bank[5][0:1, 0:64], ones[:, 0:1], C, start=True, stop=True).then_inc(count_ps, 1)

            pe.wait_ge(z_added, NB)
            pe.wait_ge(tokens_ready, 1)
            R2 = pe.value_load(rounds_sb[0:1, 1:2], min_val=1, max_val=ROUNDS)
            with pe.Fori(0, R2) as r:
                pe.wait_ge(list_in, (r + 1) * 16)
                hold(pe)
                for a in range(3):
                    ins = t.transpose(bank[6][0:CAP, 64 * a:64 * a + 64], L[:, a:a + REC * (CAP - 1) + 1:REC], ident[0:64, 0:64])
                ins.then_inc(list_ps, 1)

                def rows(u, count):
                    pe.wait_ge(xg_in[u % XG], count * 16)
                    for c in range(DC):
                        ins = t.transpose(bank[u % 2][:, c * CAP:(c + 1) * CAP], xg[u % XG][:, c:c + DC * (P - 1) + 1:DC], ident[0:CAP, 0:CAP])
                    ins.then_inc(xe_ps, 1)

                rows(0, r * GROUPS + 1)

                def group(gi, last):
                    base = r * EXPERTS + gi * RING
                    turn = r * GROUPS + gi
                    uses = (r * GROUPS + gi + 1) * 48

                    def up(u):
                        pe.wait_ge(w_in[u], uses)
                        pe.wait_ge(xe_ready, base + u + 1)
                        for a, b in ((0, 2 + u % 2), (1, 4 + u % 2)):
                            for m in range(HC):
                                for c in range(DC):
                                    ins = t.matmul(bank[b][:, m * CAP:(m + 1) * CAP], w13[:, u, a, c, m * P:(m + 1) * P],
                                                   xe[u % 2][:, c, :], start=(c == 0), stop=(c == DC - 1))
                        ins.then_inc(h_ps, 1)

                    def down(u):
                        pe.wait_ge(hT_ready, base + u + 1)
                        for m in range(HC):
                            ins = t.matmul(bank[6 + u % 2][0:CAP, :], hT[u % 2][:, m, :], w2[:, u, m, :],
                                           start=(m == 0), stop=(m == HC - 1))
                        ins.then_inc(y_ps, 1)

                    for u in range(RING):
                        if not (last and u == RING - 1):
                            rows(u + 1, turn + ((u + 1) // XG + 1))
                        up(u)
                        if u:
                            down(u - 1)
                    down(RING - 1)

                with pe.Fori(0, GROUPS - 1) as gi:
                    group(gi, False)
                group(GROUPS - 1, True)
                pe.wait_ge(y_ready, (r + 1) * EXPERTS)


_INS = ['x', 'src', 'dst', 'edge_weight', 'L0_gnn_W', 'L0_gnn_bias', 'L0_ffn_Wg', 'L0_ffn_bg', 'L0_ffn_gamma',
        'L0_ffn_beta', 'L0_ffn_W1', 'L0_ffn_b1', 'L0_ffn_W3', 'L0_ffn_b3', 'L0_ffn_W2', 'L0_ffn_b2', 'L0_ffn_gs',
        'L0_ffn_bs', 'L0_ffn_Ws1', 'L0_ffn_bs1', 'L0_ffn_Ws3', 'L0_ffn_bs3', 'L0_ffn_Ws2', 'L0_ffn_bs2']


def kernel(**inputs):
    import numpy as _np
    import concourse.bacc as _bacc
    from concourse import mybir as _mybir
    from concourse.bass_utils import run_bass_kernel_spmd as _run

    nc = _bacc.Bacc("TRN2", target_bir_lowering=False, num_devices=1)
    arrays, args = {}, []
    for name in _INS:
        a = _np.ascontiguousarray(inputs[name])
        arrays[f"in_{name}_dram"] = a
        args.append(nc.dram_tensor(f"in_{name}_dram", a.shape, _mybir.dt.from_np(a.dtype), kind="ExternalInput").ap())
    out = nc.dram_tensor("out_dram", (N, D), _mybir.dt.float32, kind="ExternalOutput").ap()
    moe_gnn(nc, *args, out)
    r = _run(nc, [arrays], core_ids=[0])
    return r.results[0]["out_dram"]
```

```python
import numpy as np
import concourse.bass as bass
from concourse import mybir
from contextlib import ExitStack

N, D = 1024, 512
EDGES = 16384
EXPERTS, HID, HS = 64, 256, 32
EPS = 1e-5
P = 128
NB = N // P
DC = D // P
HC = HID // P
TILES = EDGES // P
WIN = 16
QUAD = 4
QUADS = TILES // QUAD
SPAN = 48
TW, QW = WIN * 8, SPAN * 8
TOP = (N + WIN) * 8 - QW
POOL_M = 1
CAP = 80
ROUNDS = -(-N // CAP)
LIST = ROUNDS * CAP
REC = 2
RING = 8
GROUPS = EXPERTS // RING
XG, AHEAD = 8, 6
YS = 4
NOWHERE = 60000.0


def moe_gnn(nc, x, src, dst, ew, W, bias, Wg, bg, gamma, beta, W1, b1, W3, b3, W2, b2,
            gs, bs, Ws1, bs1, Ws3, bs3, Ws2, bs2, out):
    f32, i32, u32, bf16 = mybir.dt.float32, mybir.dt.int32, mybir.dt.uint32, mybir.dt.bfloat16
    ALU = mybir.AluOpType
    ACT = mybir.ActivationFunctionType
    AX = mybir.AxisListType.X
    ds = bass.ds

    ctx = ExitStack()
    with ctx:
        def sb(name, shape, dt=f32):
            return ctx.enter_context(nc.sbuf_tensor(name, shape, dt))

        def sem(name):
            return ctx.enter_context(nc.semaphore(name))

        nx_rows = nc.dram_tensor("nx_rows", (N, D), f32).ap()
        slots = nc.dram_tensor("slots", (EXPERTS * LIST, REC), f32).ap()
        totals = nc.dram_tensor("totals", (N + CAP, D), f32).ap()

        w13 = sb("w13", [P, RING, 2, DC, HID])
        w2 = sb("w2", [P, RING, HC, D])
        X = sb("X", [P, NB, D])
        A = sb("A", [P, (N + WIN) * 8])
        HW = sb("HW", [P, NB, D])
        GW = sb("GW", [P, DC, D])
        osl = sb("osl", [P, 2, 8, P])
        M = sb("M", [P, 2, QUAD, P])
        xh = sb("xh", [P, 2, D])
        xhT = sb("xhT", [P, 2, DC, P])
        AT = sb("AT", [P, 2, NB, P])
        eT = sb("eT", [P, 3, P])
        wrow = sb("wrow", [1, 2 * TILES + 2 * QUADS])
        neg_base = wrow[:, 0:TILES]
        tile_at = wrow[:, TILES:2 * TILES].bitcast(i32)
        quad_min = wrow[:, 2 * TILES:2 * TILES + QUADS]
        quad_at = wrow[:, 2 * TILES + QUADS:].bitcast(i32)
        rounds_sb = sb("rounds_sb", [1, 2], i32)
        ident = sb("ident", [P, P])
        ones = sb("ones", [P, P])
        iota = sb("iota", [P, P])
        spare = sb("spare", [P, 1])
        mhalf = sb("mhalf", [P, 2])
        stats = sb("stats", [P, 6 * NB])
        mv = sb("mv", [P, NB, 2])
        rstd = sb("rstd", [P, NB])
        gT = sb("gT", [P, DC, EXPERTS])
        bT = sb("bT", [P, DC, EXPERTS])
        b13T = sb("b13T", [P, 2, HC, EXPERTS])
        R = sb("R", [P, DC, P])
        bc = sb("bc", [P, P])
        gs4 = sb("gs4", [P, 2, DC])
        small = sb("small", [P, 256])
        zeros = sb("zeros", [P, 64], bf16)

        raw_wg, raw_g, raw_b = AT[0:64, 0, 0:4, :], AT[0:64, 0, 4:8, :], AT[0:64, 1, 0:4, :]
        raw_b13 = AT[0:64, 1, 4:8, :]
        edge_src, edge_dst = xhT[:, 0, 0, :].bitcast(i32), xhT[:, 0, 1, :].bitcast(i32)
        edge_w = xhT[:, 0, 2, :]
        d8 = xhT[:, 0, 3, :].bitcast(i32)
        shi = xhT[:, 1, 0, :].bitcast(i32)
        slo = xhT[:, 1, 1, :].bitcast(i32)
        key = xhT[:, 1, 2, :]
        slof = xhT[:, 1, 3, :]
        Ws = HW[:, NB - 1, 0:4 * 64].rearrange("p (c n) -> p c n", c=DC)
        Wsb = AT[:, 1, 4:6, :].rearrange("p a n -> p (a n)").rearrange("p (c n) -> p c n", c=DC)
        sentinel = HW[:, 0:5, :].rearrange("p b d -> p (b d)")[:, 0:EXPERTS * LIST * REC // P]
        Mq = [M[:, 0, :, :], M[:, 1, :, :], AT[:, 0, 0:4, :], AT[:, 0, 4:8, :]]
        lohi = M[0:1, 0, 0:2, :]
        over_row, spread_row = M[0:1, 0, 2, :], M[0:1, 0, 3, :]
        quad_max, sum_row = M[0:1, 1, 0, 0:QUADS], M[0:1, 1, 1, :]
        spread, over_most, reach, general = (M[0:1, 1, 2, i:i + 1] for i in range(4))
        reach_i = M[0:1, 1, 2, 4:5].bitcast(i32)
        biasB = M[:, 0, :, :].rearrange("p a b -> p (a b)")
        stackB = M[0:97, 1, :, :].rearrange("p a b -> p (a b)")
        route_buf = osl[:, :, :, :].rearrange("p a b c -> p (a b c)")
        nx = [route_buf[:, 512:1024], xh[:, 0, :]]
        tmp = route_buf[:, 1024:1536]
        nxT = [xhT[:, i, :, :] for i in range(2)]
        vr = route_buf[:, 1536:1664]
        er = route_buf[:, 1664:1760]
        sg = route_buf[:, 1760:1856]
        oh = [GW[:, 0, 128 * i:128 * i + 128].rearrange("p (k e) -> p k e", k=2) for i in range(2)]
        Mk = [GW[:, 1, 64 * i:64 * i + 64] for i in range(2)]
        C = GW[:, 1, 128:192]
        picked = GW[:, 1, 192:320].rearrange("p (k e) -> p k e", k=2)
        hsig = GW[:, 1, 320:352]
        slot = GW[:, 1, 352:352 + 2 * NB].bitcast(i32).rearrange("p (s k) -> p s k", k=2)
        weighted = GW[:, 1, 384:448]
        stack = [route_buf[:, 128 * i:128 * i + 97] for i in range(2)]
        before = GW[:, 0, 256:384]
        stackT = [GW[0:97, 2 + i // 4, 128 * (i % 4):128 * (i % 4) + 128] for i in range(NB)]
        late = A[:, :]
        xg = [late[0:CAP, 512 * i:512 * i + 512] for i in range(XG)]
        o = 512 * XG
        ysb = [late[0:CAP, o + 512 * i:o + 512 * i + 512] for i in range(YS)]
        o += 512 * YS
        xe = [late[:, o + 320 * i:o + 320 * i + 320].rearrange("p (c t) -> p c t", c=DC) for i in range(2)]
        o += 640
        sl = [late[:, o + 160 * i:o + 160 * i + 160].rearrange("p (m t) -> p m t", m=HC) for i in range(2)]
        o += 320
        hT = [late[:, o + 160 * i:o + 160 * i + 160].rearrange("p (m t) -> p m t", m=HC) for i in range(2)]
        o += 320
        L = late[0:EXPERTS, o:o + CAP * REC]
        o += CAP * REC
        TOK = late[0:CAP, o:o + 64].bitcast(i32)
        DROW = late[0:CAP, o + 64:o + 128].bitcast(i32)
        CW = late[0:CAP, o + 128:o + 192]
        idx_g = late[0:CAP, o + 192:o + 192 + RING + AHEAD].bitcast(i32)
        idx_s = late[0:CAP, o + 208:o + 208 + RING].bitcast(i32)
        mv1 = small[:, 0:16].rearrange("p (s a) -> p s a", a=2)
        ve = small[:, 16:32].rearrange("p (s a) -> p s a", a=2)
        rs = small[:, 32:48].rearrange("p (s a) -> p s a", a=2)
        nm, ratio = small[:, 48:56], small[:, 56:64]
        m8, i8 = small[:, 88:96], small[:, 96:104].bitcast(u32)
        idf = [small[:, 104 + 2 * i:106 + 2 * i] for i in range(2)]
        ssum, rsum = small[:, 108:109], small[:, 109:110]
        pos = small[:, 114:116]
        key8 = [small[:, 120 + 32 * i:128 + 32 * i] for i in range(2)]
        w8 = [small[:, 128 + 32 * i:136 + 32 * i] for i in range(2)]
        rec = small[:, 192:192 + NB * 2 * REC].rearrange("p (s k a) -> p s k a", k=2, a=REC)
        mn, mx = small[:, 136:137], small[:, 137:138]
        st6 = small[:, 142:148]
        rowz = GW[0:1, 0, 384:448]
        caps = rowz[0:1, 0:ROUNDS]
        over = rowz[0:1, 16:16 + ROUNDS]
        most, nround = rowz[0:1, 32:33], rowz[0:1, 33:34]
        var_eps = small[:, 64:72]

        bank = [ctx.enter_context(nc.psum_tensor(f"bank{i}", [P, 512], f32)) for i in range(8)]

        route_bank = [bank[7]] * (NB - 1) + [bank[0]]
        z_bank = [bank[i] for i in (2, 3, 4, 2, 4, 3, 5, 7)]

        edges_in, gw_in, raw_in, small_in, ws_in = (sem(s) for s in (
            "edges_in", "gw_in", "raw_in", "small_in", "ws_in"))
        x_in = [sem(f"x_in{i}") for i in range(4)]
        late_in = sem("late_in")
        consts = sem("consts")
        sentinel_out = sem("sentinel_out")
        dve_chain = sem("dve_chain")
        pool_chain = sem("pool_chain")
        edge_prepped = sem("edge_prepped")
        edges_transposed = sem("edges_transposed")
        edges_ready = sem("edges_ready")
        slo_ready, base_ready, base_ps = sem("slo_ready"), sem("base_ready"), sem("base_ps")
        raw_transposed = sem("raw_transposed")
        raw_evac = sem("raw_evac")
        wsb_ready = sem("wsb_ready")
        sums_done = sem("sums_done")
        stats_ready = sem("stats_ready")
        rstd_ready = sem("rstd_ready")
        xh_ready = sem("xh_ready")
        xhT_ps = sem("xhT_ps")
        xhT_ready = sem("xhT_ready")
        hw_ps = sem("hw_ps")
        hw_ready = sem("hw_ready")
        key_copied, osl_chain, m_pool = sem("key_copied"), sem("osl_chain"), sem("m_pool")
        osl_ready = sem("osl_ready")
        m_ready = sem("m_ready")
        quad_done = [sem("first_quad_done"), sem("second_quad_done")]
        a_chain = sem("a_chain")
        win_chain = sem("win_chain")
        at_ps = sem("at_ps")
        at_ready = sem("at_ready")
        out_ps = sem("out_ps")
        x1_ready = sem("x1_ready")
        mv1_ready, nm_ready, ratio_ready, nx_ready = (sem(s) for s in (
            "mv1_ready", "nm_ready", "ratio_ready", "nx_ready"))
        nx_out = [sem(f"nx_out{i}") for i in range(2)]
        nxT_ps, nxT_ready = sem("nxT_ps"), sem("nxT_ready")
        route_ps, vr_ready, er_ready = sem("route_ps"), sem("vr_ready"), sem("er_ready")
        stack_ready, rank_ps, stackT_ready = (sem(s) for s in (
            "stack_ready", "rank_ps", "stackT_ready"))
        z_ps, z_added = sem("z_ps"), sem("z_added")
        rec_ready = sem("rec_ready")
        rec_out = [sem(f"rec_out{i}") for i in range(2)]
        tokens_ready = sem("tokens_ready")
        xg_clear = sem("xg_clear")
        w_in = [sem(f"w_in{i}") for i in range(RING)]
        list_in, list_ps, list_ready = sem("list_in"), sem("list_ps"), sem("list_ready")
        idx_copied = sem("idx_copied")
        xg_in = [sem(f"xg_in{i}") for i in range(XG)]
        xe_ps, xe_ready, h_ps, sl_ready, hT_ready, y_ps, y_ready = (sem(s) for s in (
            "xe_ps", "xe_ready", "h_ps", "sl_ready", "hT_ready", "y_ps", "y_ready"))
        y_out = [sem(f"y_out{i}") for i in range(YS)]
        x_out = sem("x_out")
        out_done = sem("out_done")
        held = sem("held")

        def hold(engine):
            engine.sem_inc(held, 1)

        W1v = W1.rearrange("e (p c) h -> e p (c h)", c=DC)
        W3v = W3.rearrange("e (p c) h -> e p (c h)", c=DC)
        W2v = W2.rearrange("e (m p) d -> e p m d", p=P)
        block = ctx.enter_context(nc.Block())

        @block.sync
        def _(sp):
            edge_view = [a.rearrange("(t p) -> t p", p=P) for a in (dst, src, ew)]
            for to, a in zip((edge_dst, edge_src, edge_w), edge_view):
                sp.dma_start(to, a).then_inc(edges_in, 16)
            xv = x.rearrange("(b p) d -> p b d", p=P)
            sp.dma_start(X[:, 0:2, :], xv[:, 0:2, :]).then_inc(x_in[0], 16)
            v3 = "e (c d) -> e c d"
            for to, a in ((raw_wg, Wg), (raw_g, gamma), (raw_b, beta)):
                sp.dma_start(to, a.rearrange(v3, c=4)).then_inc(raw_in, 16)
            sp.dma_start(raw_b13[:, 0:2, :], b1.rearrange(v3, c=HC)).then_inc(raw_in, 16)
            sp.dma_start(raw_b13[:, 2:4, :], b3.rearrange(v3, c=HC)).then_inc(raw_in, 16)
            sp.dma_start(gs4[:, 0, :], gs.rearrange("(p c) -> p c", c=DC)).then_inc(small_in, 16)
            sp.dma_start(gs4[:, 1, :], bs.rearrange("(p c) -> p c", c=DC)).then_inc(small_in, 16)
            sp.dma_start(bc[:, 0:64], bg.partition_broadcast(P)).then_inc(small_in, 16)
            sp.dma_start(bc[:, 64:96], bs1.partition_broadcast(P)).then_inc(small_in, 16)
            sp.dma_start(bc[:, 96:128], bs3.partition_broadcast(P)).then_inc(small_in, 16)
            sp.dma_start(Ws[:, :, 0:32], Ws1.rearrange("(p c) n -> p c n", c=DC)).then_inc(ws_in, 16)
            sp.dma_start(Ws[:, :, 32:64], Ws3.rearrange("(p c) n -> p c n", c=DC)).then_inc(ws_in, 16)
            for i in range(1, 4):
                sp.dma_start(X[:, 2 * i:2 * i + 2, :], xv[:, 2 * i:2 * i + 2, :]).then_inc(x_in[i], 16)
            sp.dma_start(GW[:, :, :], W.rearrange("(p c) n -> p c n", c=DC)).then_inc(gw_in, 16)
            sp.wait_ge(consts, 6)
            sp.dma_start(slots.rearrange("(p n) r -> p (n r)", p=P), sentinel).then_inc(sentinel_out, 16)
            sp.dma_start(totals[N:N + CAP, :], HW[0:CAP, 0, :]).then_inc(sentinel_out, 16)

            def load_expert(e, u):
                sp.dma_start(w13[:, u, 0, :, :].rearrange("p c h -> p (c h)"), W1v[e]).then_inc(w_in[u], 16)
                sp.dma_start(w13[:, u, 1, :, :].rearrange("p c h -> p (c h)"), W3v[e]).then_inc(w_in[u], 16)
                sp.dma_start(w2[:, u, :, :], W2v[e]).then_inc(w_in[u], 16)

            for u in range(RING):
                load_expert(u, u)
            sp.wait_ge(edges_ready, 3)
            sp.dma_start(biasB, bias.partition_broadcast(P)).then_inc(late_in, 16)
            sp.dma_start(stackB[0:64, :], b2).then_inc(late_in, 16)
            sp.dma_start(stackB[64:96, :], Ws2).then_inc(late_in, 16)
            sp.dma_start(stackB[96:97, :], bs2.unsqueeze(0)).then_inc(late_in, 16)
            for s in range(NB):
                sp.wait_ge(nx_ready, s + 1)
                sp.dma_start(nx_rows[s * P:(s + 1) * P, :], nx[s % 2]).then_inc(nx_out[s % 2], 16)
            sp.wait_ge(tokens_ready, 1)
            R2 = sp.value_load(rounds_sb[0:1, 1:2], min_val=1, max_val=ROUNDS)
            for i in range(2):
                sp.wait_ge(rec_out[i], 32 * NB // 2)
            lists = slots.rearrange("(e n) r -> e (n r)", e=EXPERTS)

            def store_x(blocks):
                for s in blocks:
                    sp.wait_ge(z_added, s + 1)
                    sp.dma_start(totals[s * P:(s + 1) * P, :], X[:, s, :]).then_inc(x_out, 16)

            with sp.Fori(0, R2) as r:
                sp.dma_start(L, lists[:, ds(r * (CAP * REC), CAP * REC)]).then_inc(list_in, 16)
                with sp.If(r < 1):
                    store_x(range(NB))
                with sp.Fori(0, GROUPS - 1) as g:
                    for u in range(RING):
                        used = sp.snap(r * EXPERTS + g * RING + (u + 1))
                        e = sp.snap(g * RING + (RING + u))
                        sp.wait_ge(y_ps, used)
                        load_expert(e, u)
                with sp.If(r + 1 < R2):
                    for u in range(RING):
                        used = sp.snap(r * EXPERTS + (EXPERTS - RING + u + 1))
                        sp.wait_ge(y_ps, used)
                        load_expert(u, u)
            last = sp.snap(R2 * (16 * EXPERTS // YS))
            for i in range(YS):
                sp.wait_ge(y_out[i], last)
            sp.dma_start(out.rearrange("(p b) d -> p (b d)", p=P),
                         totals[0:N, :].rearrange("(p b) d -> p (b d)", p=P)).then_inc(out_done, 16)
            sp.wait_ge(out_done, 16)

        @block.gpsimd
        def _(pool):
            g = nc.gpsimd
            g.memset(ones[:, :], 1.0).then_inc(consts, 1)
            pool.wait_ge(consts, 1)
            g.affine_select(out=ident[:, :], in_=ones[:, :], pattern=[[-1, P]], compare_op=ALU.is_equal,
                            fill=0.0, base=0, channel_multiplier=1).then_inc(consts, 1)
            g.iota(iota[:, :], pattern=[[1, P]], base=0, channel_multiplier=0,
                   allow_small_or_imprecise_dtypes=True).then_inc(consts, 1)
            g.iota(spare[:, :], pattern=[[1, 1]], base=N, channel_multiplier=1,
                   allow_small_or_imprecise_dtypes=True).then_inc(consts, 1)
            g.memset(zeros[:, :], 0.0)
            g.memset(mhalf[:, :], -0.5).then_inc(consts, 1)
            g.memset(sentinel, NOWHERE).then_inc(consts, 1)
            g.memset(rec, 0.0).then_inc(consts, 1)
            pool.wait_ge(consts, 7)
            g.iota(rec[:, :, :, 0], pattern=[[P, NB], [0, 2]], base=0, channel_multiplier=1,
                   allow_small_or_imprecise_dtypes=True).then_inc(consts, 1)
            pool_n = [0]

            def link(ins):
                pool_n[0] += 1
                ins.then_inc(pool_chain, 1)
                pool.wait_ge(pool_chain, pool_n[0])

            def inverse_deviations(blocks, n):
                pool.wait_ge(stats_ready, n)
                c = slice(blocks[0], blocks[-1] + 1)
                link(g.tensor_scalar(var_eps[:, c], mv[:, c, 1], EPS, None, ALU.add))
                g.tensor_tensor(rstd[:, c], var_eps[:, c], mhalf[:, 0:1].broadcast_to([P, len(blocks)]), ALU.pow).then_inc(rstd_ready, 1)

            inverse_deviations(range(0, 2), 1)
            pool.wait_ge(edges_ready, 1)
            R1 = pool.value_load(rounds_sb[0:1, 0:1], min_val=1, max_val=N // WIN)

            def pair(r, j, first):
                half = (r * (NB // 2) + j) * 4
                for h in range(4):
                    if not first or h >= 2:
                        pool.wait_ge(m_pool, (half + (h - 1)) * 2)
                        hold(pool)
                    g.tensor_copy(key8[h % 2], eT[:, 0, ds(j * 32 + 8 * h, 8)]).then_inc(key_copied, 1)
                    g.tensor_copy(w8[h % 2], eT[:, 2, ds(j * 32 + 8 * h, 8)]).then_inc(key_copied, 1)
                    pool.wait_ge(key_copied, (half + (h + 1)) * 2)
                    for q in (2 * h, 2 * h + 1):
                        if not first or q >= 4:
                            pool.wait_ge(quad_done[q % 2], half + (q // 2 - 1))
                        elif q == 2:
                            pool.wait_ge(raw_transposed, 2)
                        hold(pool)
                        for k in range(POOL_M):
                            t = (q % 2) * QUAD + k
                            ins = g.tensor_scalar(Mq[q % 4][:, k, :], iota[:, :], key8[h % 2][:, t:t + 1], w8[h % 2][:, t:t + 1],
                                                  ALU.is_equal, ALU.mult)
                        ins.then_inc(m_pool, 1)

            pair(0, 0, True)
            inverse_deviations(range(2, NB), 2)
            pool.wait_ge(small_in, 80)
            pool.wait_ge(ws_in, 32)
            pool.wait_ge(raw_transposed, 2)
            for c in range(DC):
                g.tensor_scalar(R[:, c, 64:128], Ws[:, c, :], gs4[:, 0, c:c + 1], None, ALU.mult)
                ins = g.tensor_scalar(Wsb[:, c, :], Ws[:, c, :], gs4[:, 1, c:c + 1], None, ALU.mult)
            ins.then_inc(wsb_ready, 1)
            with pool.Fori(1, NB // 2) as j:
                pair(0, j, False)
            with pool.If(R1 > 1):
                with pool.Fori(1, R1) as r:
                    pool.wait_ge(win_chain, r * 6)
                    hold(pool)
                    with pool.Fori(0, NB // 2) as j:
                        pair(r, j, False)
            def scatter_records(s):
                pool.wait_ge(rec_ready, s + 1)
                if s == 0:
                    pool.wait_ge(sentinel_out, 32)
                for k in range(2):
                    g.indirect_dma_start(slots, bass.IndirectOffsetOnAxis(ap=slot[:, s, k:k + 1], axis=0),
                                         rec[:, s, k, :], None).then_inc(rec_out[s % 2], 16)

            pool.wait_ge(edges_ready, 3)
            link(g.affine_select(out=before, in_=ones[:, :], pattern=[[1, P]], compare_op=ALU.is_gt,
                                 fill=0.0, base=0, channel_multiplier=-1))
            for s in range(NB + 2):
                if s < NB:
                    pool.wait_ge(mv1_ready, s + 1)
                    g.tensor_scalar(ve[:, s, 0:1], mv1[:, s, 1:2], 1.0 + EPS, EPS * EPS, ALU.mult, ALU.add)
                    link(g.tensor_scalar(ve[:, s, 1:2], mv1[:, s, 1:2], EPS, None, ALU.add))
                    link(g.tensor_tensor(rs[:, s, :], ve[:, s, :], mhalf[:, :], ALU.pow))
                    link(g.tensor_tensor(nm[:, s:s + 1], mv1[:, s, 0:1], rs[:, s, 0:1], ALU.mult))
                    g.tensor_scalar(nm[:, s:s + 1], nm[:, s:s + 1], -1.0, None, ALU.mult).then_inc(nm_ready, 1)
                    link(g.tensor_tensor(ratio[:, s:s + 1], ve[:, s, 0:1], rs[:, s, 0:1], ALU.mult))
                    g.tensor_tensor(ratio[:, s:s + 1], ratio[:, s:s + 1], rs[:, s, 1:2], ALU.mult).then_inc(ratio_ready, 1)
                if s == NB - 1:
                    pool.wait_ge(at_ps, 2 * NB)
                    g.memset(late[0:CAP, 0:512 * XG], 0.0).then_inc(xg_clear, 1)
                if s >= 2:
                    scatter_records(s - 2)
            pool.wait_ge(xg_clear, 1)
            pool.wait_ge(nx_out[0], 16 * NB // 2)
            pool.wait_ge(nx_out[1], 16 * NB // 2)
            pool.wait_ge(tokens_ready, 1)
            R2 = pool.value_load(rounds_sb[0:1, 1:2], min_val=1, max_val=ROUNDS)

            def gather(col, b):
                g.indirect_dma_start(xg[b], None, nx_rows, bass.IndirectOffsetOnAxis(ap=idx_g[:, col:col + 1], axis=0),
                                     bounds_check=N - 1, oob_is_err=False).then_inc(xg_in[b], 16)

            def scatter(u, count, before):
                pool.wait_ge(y_ready, count)
                if u:
                    pool.wait_ge(y_out[(u - 1) % YS], (before + (u - 1) // YS + 1) * 16)
                hold(pool)
                g.indirect_dma_start(totals, bass.IndirectOffsetOnAxis(ap=idx_s[:, u:u + 1], axis=0), ysb[u % YS], None,
                                     compute_op=ALU.add).then_inc(y_out[u % YS], 16)

            with pool.Fori(0, R2) as r:
                pool.wait_ge(list_ready, r + 1)
                hold(pool)
                g.tensor_copy(idx_g[:, 0:AHEAD], TOK[:, 0:AHEAD]).then_inc(idx_copied, 1)
                pool.wait_ge(idx_copied, r * (2 * GROUPS + 1) + 1)
                hold(pool)
                for u in range(AHEAD):
                    gather(u, u)

                def group(gi, first, last):
                    n = RING if last else RING + AHEAD
                    base = r * EXPERTS + gi * RING
                    before = r * (EXPERTS // YS) + gi * (RING // YS)
                    for b in range(AHEAD):
                        pool.wait_ge(xg_in[b], (r * GROUPS + gi + 1) * 16)
                    hold(pool)
                    g.tensor_copy(idx_g[:, 0:n], TOK[:, ds(gi * RING, n)]).then_inc(idx_copied, 1)
                    if first:
                        pool.wait_ge(x_out, 16 * NB)
                        hold(pool)
                    else:
                        for b in range(YS):
                            pool.wait_ge(y_out[b], before * 16)
                        hold(pool)
                    g.tensor_copy(idx_s[:, :], DROW[:, ds(gi * RING, RING)]).then_inc(idx_copied, 1)
                    pool.wait_ge(idx_copied, r * (2 * GROUPS + 1) + gi * 2 + 3)
                    hold(pool)
                    for u in range(RING):
                        if not (last and u >= RING - AHEAD):
                            if not first or u + AHEAD >= XG:
                                pool.wait_ge(xe_ps, base + (u + AHEAD - XG + 1))
                                hold(pool)
                            gather(u + AHEAD, (u + AHEAD) % XG)
                        if u:
                            scatter(u - 1, base + u, before)
                    scatter(RING - 1, base + RING, before)

                group(0, True, False)
                with pool.Fori(1, GROUPS - 1) as gi:
                    group(gi, False, False)
                group(GROUPS - 1, False, True)
                for b in range(YS):
                    pool.wait_ge(y_out[b], (r + 1) * (16 * EXPERTS // YS))

        @block.scalar
        def _(act):
            a = nc.scalar
            a.memzero(A[:, :]).then_inc(a_chain, 4)

            def one_hots(half, j, h, first):
                if not first or h >= 2:
                    act.wait_ge(quad_done[1], half + (h - 1))
                for k in range(8):
                    ins = a.activation(osl[:, h % 2, k, :], iota[:, :], ACT.Abs, bias=eT[:, 1, ds(j * 32 + 8 * h + k, 1)])
                ins.then_inc(osl_chain, 1)
                act.wait_ge(osl_chain, half + (h + 1))
                a.activation(osl[:, h % 2, :, :], osl[:, h % 2, :, :], ACT.Relu, scale=-1.0, bias=1.0).then_inc(osl_ready, 1)

            def x_transposed(g, u):
                act.wait_ge(xhT_ps, g + 1)
                a.copy(xhT[:, u, :, :].rearrange("p c n -> p (c n)"), bank[4 + u][:, :]).then_inc(xhT_ready, 1)

            def x_times_w(g, u):
                act.wait_ge(hw_ps, g + 1)
                act.wait_ge(sentinel_out, 32)
                a.copy(HW[:, ds(g, 1), :].rearrange("p a n -> p (a n)"), bank[6 + u][:, :]).then_inc(hw_ready, 1)

            def pair(j, last):
                half = j * 4
                x_transposed(j * 2, 0)
                one_hots(half, j, 2, False)
                one_hots(half, j, 3, False)
                x_times_w(j * 2, 0)
                x_transposed(j * 2 + 1, 1)
                if not last:
                    one_hots(half + 4, j + 1, 0, False)
                    one_hots(half + 4, j + 1, 1, False)
                    x_times_w(j * 2 + 1, 1)

            act.wait_ge(slo_ready, 1)
            one_hots(0, 0, 0, True)
            act.wait_ge(raw_transposed, 1)
            a.copy(R[:, :, 0:64], bank[2][:, 0:256].rearrange("p (c e) -> p c e", c=DC)).then_inc(raw_evac, 1)
            a.copy(gT[:, :, :].rearrange("p c e -> p (c e)"), bank[2][:, 256:512]).then_inc(raw_evac, 1)
            act.wait_ge(raw_transposed, 2)
            a.copy(bT[:, :, :].rearrange("p c e -> p (c e)"), bank[3][:, 0:256]).then_inc(raw_evac, 1)
            a.copy(b13T[:, :, :, :].rearrange("p a m e -> p (a m e)"), bank[3][:, 256:512]).then_inc(raw_evac, 1)
            one_hots(0, 0, 1, True)
            act.wait_ge(edges_ready, 1)
            R1 = act.value_load(rounds_sb[0:1, 0:1], min_val=1, max_val=N // WIN)
            with act.Fori(0, NB // 2 - 1) as j:
                pair(j, False)
            pair(NB // 2 - 1, True)
            act.wait_ge(wsb_ready, 1)
            x_times_w(NB - 1, 1)
            with act.If(R1 > 1):
                with act.Fori(1, R1) as r:
                    with act.Fori(0, NB // 2) as j:
                        for h in range(4):
                            one_hots((r * (NB // 2) + j) * 4, j, h, False)

            def copy_a(s):
                if s >= 2:
                    act.wait_ge(out_ps, s - 1)
                for k in range(2):
                    act.wait_ge(at_ps, 2 * s + k + 1)
                    a.copy(AT[:, s % 2, 4 * k:4 * k + 4, :].rearrange("p k n -> p (k n)"),
                           bank[2 * (s % 2) + k][:, :]).then_inc(at_ready, 1)

            copy_a(0)
            for s in range(NB + 2):
                if s + 1 < NB:
                    copy_a(s + 1)
                if s >= 2:
                    act.wait_ge(vr_ready, s - 1)
                    a.activation(er, er, ACT.Exp, scale=-1.0).then_inc(er_ready, 1)
                if 1 <= s <= NB:
                    t = s - 1
                    act.wait_ge(nm_ready, t + 1)
                    if t >= 2:
                        act.wait_ge(nx_out[t % 2], 16 * (t // 2))
                        act.wait_ge(nxT_ps, t - 1)
                    a.activation(nx[t % 2], X[:, t, :], ACT.Identity, scale=rs[:, t, 0:1], bias=nm[:, t:t + 1]).then_inc(nx_ready, 1)
                    act.wait_ge(nxT_ps, t + 1)
                    if t >= 2:
                        act.wait_ge(route_ps, t - 1)
                    a.copy(nxT[t % 2].rearrange("p c n -> p (c n)"), bank[6][:, :]).then_inc(nxT_ready, 1)
            act.wait_ge(tokens_ready, 1)
            R2 = act.value_load(rounds_sb[0:1, 1:2], min_val=1, max_val=ROUNDS)
            with act.Fori(0, R2) as r:
                def group(g, first):
                    base = r * EXPERTS + g * RING

                    def silu(u):
                        act.wait_ge(h_ps, base + u + 1)
                        for m in range(HC):
                            ins = a.activation(sl[u % 2][:, m, :], bank[2 + u % 2][:, m * CAP:(m + 1) * CAP], ACT.Silu,
                                               bias=b13T[:, 0, m, ds(g * RING + u, 1)])
                        ins.then_inc(sl_ready, 1)

                    def result(u):
                        act.wait_ge(y_ps, base + u + 1)
                        if not first or u >= YS:
                            act.wait_ge(y_out[u % YS], (r * (EXPERTS // YS) + g * (RING // YS) + u // YS) * 16)
                        a.activation(ysb[u % YS], bank[6 + u % 2][0:CAP, :], ACT.Copy,
                                     scale=CW[:, ds(g * RING + u, 1)]).then_inc(y_ready, 1)

                    for u in range(RING):
                        silu(u)
                        if u:
                            result(u - 1)
                    result(RING - 1)

                act.wait_ge(list_ready, r + 1)
                group(0, True)
                with act.Fori(1, GROUPS) as g:
                    group(g, False)

        @block.vector
        def _(dve):
            v = nc.vector
            chain = [0]

            def link(ins):
                chain[0] += 1
                ins.then_inc(dve_chain, 1)
                dve.wait_ge(dve_chain, chain[0])

            def mark(ins):
                chain[0] += 1
                ins.then_inc(dve_chain, 1)
                return chain[0]

            def need(*marks):
                dve.wait_ge(dve_chain, max(marks))

            def mean_and_variance(blocks):
                for b in blocks:
                    if b % 2 == 0:
                        dve.wait_ge(x_in[b // 2], 16)
                    c_st = mark(v.bn_stats(stats[:, 6 * b:6 * b + 6], X[:, b, :]))
                need(c_st)
                for b in blocks:
                    ins = v.bn_aggr(mv[:, b, :], stats[:, 6 * b:6 * b + 6])
                ins.then_inc(stats_ready, 1)

            dve.wait_ge(edges_in, 48)
            c_d8 = mark(v.tensor_scalar(d8, edge_dst, 3, None, ALU.arith_shift_left))
            c_hi = mark(v.tensor_scalar(shi, edge_src, 7, None, ALU.arith_shift_right))
            c_lo = mark(v.tensor_scalar(slo, edge_src, P - 1, None, ALU.bitwise_and))
            need(c_d8)
            mark(v.tensor_reduce(mn, d8, AX, ALU.min))
            mark(v.tensor_reduce(mx, d8, AX, ALU.max))
            need(c_hi)
            mark(v.tensor_tensor(key, d8, shi, ALU.add))
            need(c_lo)
            v.tensor_scalar(slof, slo, -1.0, None, ALU.mult).then_inc(edge_prepped, 1)
            mean_and_variance(range(0, 2))
            dve.wait_ge(edges_transposed, 1)
            by_quad = lambda a: a.rearrange("a (q k) -> a q k", k=QUAD)
            of_quad = lambda a: a.unsqueeze(2).broadcast_to([1, QUADS, QUAD])
            mn_row, mx_row = lohi[:, 0, :], lohi[:, 1, :]
            c_row = mark(v.tensor_copy(lohi.rearrange("a b t -> a (b t)"), bank[1][0:1, 0:2 * P]))
            v.tensor_copy(eT[:, :, :].rearrange("p a t -> p (a t)"), bank[0][:, 0:3 * P]).then_inc(slo_ready, 1)
            need(c_row)
            c_min = mark(v.tensor_reduce(quad_min, by_quad(mn_row), AX, ALU.min))
            c_max = mark(v.tensor_reduce(quad_max, by_quad(mx_row), AX, ALU.max))
            c_spr = mark(v.tensor_tensor(spread_row, mx_row, mn_row, ALU.subtract))
            need(c_min)
            c_over = mark(v.tensor_tensor(by_quad(over_row), by_quad(mn_row), of_quad(quad_min), ALU.subtract))
            need(c_max)
            c_sum = mark(v.tensor_tensor(quad_max, quad_max, quad_min, ALU.subtract))
            need(c_spr)
            c_s = mark(v.tensor_reduce(spread, spread_row, AX, ALU.max))
            need(c_over)
            c_o = mark(v.tensor_reduce(over_most, over_row, AX, ALU.max))
            need(c_sum)
            mark(v.tensor_reduce(reach, quad_max, AX, ALU.max))
            need(c_s, c_o)
            link(v.tensor_scalar(general, spread, float(TW), None, ALU.is_ge))
            link(v.scalar_tensor_tensor(general, over_most, float(QW - TW), general, ALU.is_gt, ALU.max))
            v.scalar_tensor_tensor(neg_base, over_row, general, mn_row, ALU.mult, ALU.subtract).then_inc(base_ready, 1)
            c_at = mark(v.tensor_scalar(quad_at, quad_min, float(TOP), None, ALU.min))
            c_re = mark(v.tensor_tensor(reach_i, reach, general, ALU.mult))
            need(c_at)
            dve.wait_ge(base_ready, 1)
            c_t = mark(v.scalar_tensor_tensor(by_quad(sum_row), by_quad(neg_base), -1.0, of_quad(quad_at), ALU.mult, ALU.subtract))
            need(c_re)
            link(v.tensor_scalar(reach_i, reach_i, 7, None, ALU.arith_shift_right))
            mark(v.tensor_scalar(rounds_sb[0:1, 0:1], reach_i, 1.0, None, ALU.add))
            link(v.tensor_scalar(tile_at, sum_row, float(QW - TW), None, ALU.min))
            dve.wait_ge(slo_ready, 1)
            dve.wait_ge(base_ps, 1)
            v.tensor_tensor(eT[:, 0, :], eT[:, 0, :], bank[1][:, 384:512], ALU.add).then_inc(edges_ready, 1)
            dve.wait_ge(edges_ready, 1)
            R1 = dve.value_load(rounds_sb[0:1, 0:1], min_val=1, max_val=N // WIN)

            BEHIND = 3

            def sums(r, j, q):
                done = dve.snap((r * (NB // 2) + j) * 4)
                at = dve.value_load(quad_at[0:1, ds(j * 8 + q, 1)], min_val=0, max_val=TOP)
                to = A[:, ds(at, QW)]
                dve.wait_ge(quad_done[q % 2], done + (q // 2 + 1))
                dve.wait_ge(a_chain, done * 2 + (q + 4))
                v.tensor_tensor(to, to, bank[q % 4][:, 0:QW], ALU.add).then_inc(a_chain, 1)

            def sum_pair(r, j, with_x, first):
                for q in range(8):
                    if with_x and q < 2:
                        b = j * 2 + q
                        if first or q == 0:
                            dve.wait_ge(rstd_ready, 1 if first else 2)
                        v.tensor_scalar(xh[:, q, :], X[:, ds(b, 1), :].rearrange("p a n -> p (a n)"),
                                        mv[:, ds(b, 1), 0], rstd[:, ds(b, 1)],
                                        ALU.subtract, ALU.mult).then_inc(xh_ready, 1)
                    if first and q == 2:
                        dve.wait_ge(raw_transposed, 2)
                    for k in range(POOL_M, QUAD):
                        t = j * 32 + (QUAD * q + k)
                        ins = v.tensor_scalar(Mq[q % 4][:, k, :], iota[:, :], eT[:, 0, ds(t, 1)], eT[:, 2, ds(t, 1)],
                                              ALU.is_equal, ALU.mult)
                    ins.then_inc(m_ready, 1)
                    if with_x and first and q == 1:
                        mean_and_variance(range(2, NB))
                    if q >= BEHIND:
                        sums(r, j, q - BEHIND)
                    elif not first:
                        sums(r, j - 1, q - BEHIND + 8)

            def all_pairs(r, with_x):
                sum_pair(r, 0, with_x, True)
                with dve.Fori(1, NB // 2) as j:
                    sum_pair(r, j, with_x, False)
                for q in range(8 - BEHIND, 8):
                    sums(r, NB // 2 - 1, q)

            all_pairs(0, True)
            more = dve.snap(R1)
            with dve.If(more > 1):
                with dve.Fori(1, R1) as r:
                    w = dve.snap(r * 6)
                    v.tensor_scalar(eT[:, 0, :], eT[:, 0, :], float(P), None, ALU.subtract).then_inc(win_chain, 1)
                    v.tensor_scalar(neg_base, neg_base, float(TW), None, ALU.subtract).then_inc(win_chain, 1)
                    v.tensor_scalar(quad_min, quad_min, float(TW), None, ALU.add).then_inc(win_chain, 1)
                    dve.wait_ge(win_chain, w - 3)
                    v.tensor_scalar(quad_at, quad_min, float(TOP), None, ALU.min).then_inc(win_chain, 1)
                    dve.wait_ge(win_chain, w - 2)
                    v.scalar_tensor_tensor(by_quad(sum_row), by_quad(neg_base), -1.0, of_quad(quad_at),
                                           ALU.mult, ALU.subtract).then_inc(win_chain, 1)
                    dve.wait_ge(win_chain, w - 1)
                    v.tensor_scalar(tile_at, sum_row, float(QW - TW), None, ALU.min).then_inc(win_chain, 1)
                    dve.wait_ge(win_chain, w)
                    hold(dve)
                    all_pairs(r, False)
            dve.wait_ge(a_chain, R1 * QUADS + 4)
            dve.wait_ge(hw_ps, NB)
            dve.wait_ge(sums_done, 1)
            link(v.tensor_tensor(bc[:, 64:128], bc[:, 64:128], bank[7][:, 0:64], ALU.add))
            v.memset(C, 0.0).then_inc(edges_ready, 1)
            dve.wait_ge(edges_ready, 2)
            for i in range(2):
                ins = v.memset(stack[i][:, 96:97], 1.0)
            ins.then_inc(edges_ready, 1)

            def relu_add(s):
                dve.wait_ge(out_ps, s + 1)
                if s == 0:
                    dve.wait_ge(late_in, 64)
                link(v.tensor_tensor(tmp, bank[4 + s % 2][:, :], biasB, ALU.add))
                v.scalar_tensor_tensor(X[:, s, :], tmp, 0.0, X[:, s, :], ALU.max, ALU.add).then_inc(x1_ready, 1)
                dve.wait_ge(x1_ready, s + 1)
                link(v.bn_stats(st6, X[:, s, :]))
                v.bn_aggr(mv1[:, s, :], st6).then_inc(mv1_ready, 1)

            def route(t):
                i = t % 2
                cw = rec[:, t, :, 1]
                dve.wait_ge(route_ps, t + 1)
                dve.wait_ge(ratio_ready, t + 1)
                mark(v.tensor_tensor(vr[:, 64:128], route_bank[t][:, 64:128], bc[:, 64:128], ALU.add))
                link(v.scalar_tensor_tensor(vr[:, 0:64], route_bank[t][:, 0:64], ratio[:, t:t + 1], bc[:, 0:64], ALU.mult, ALU.add))
                v.tensor_scalar(er, vr[:, 0:96], -87.0, None, ALU.max).then_inc(vr_ready, 1)
                dve.wait_ge(er_ready, t + 1)
                link(v.tensor_scalar(er, er, 1.0, None, ALU.add))
                link(v.reciprocal(sg, er))
                c_m8 = mark(v.max(m8, sg[:, 0:64]))
                c_hs = mark(v.tensor_tensor(hsig, vr[:, 64:96], sg[:, 64:96], ALU.mult))
                need(c_m8)
                c_i8 = mark(v.max_index(i8, m8, sg[:, 0:64]))
                c_ss = mark(v.tensor_tensor(ssum, m8[:, 0:1], m8[:, 1:2], ALU.add))
                need(c_hs, c_i8)
                c_id = mark(v.tensor_copy(idf[i], i8[:, 0:2]))
                mark(v.tensor_tensor(stack[i][:, 64:96], hsig, vr[:, 96:128], ALU.mult))
                need(c_ss, c_id)
                c_rs = mark(v.reciprocal(rsum, ssum))
                c_oh = mark(v.tensor_tensor(oh[i], iota[:, 0:64].unsqueeze(1).broadcast_to([P, 2, 64]),
                                            idf[i].unsqueeze(2).broadcast_to([P, 2, 64]), ALU.is_equal))
                need(c_rs)
                c_cw = mark(v.tensor_scalar(cw, m8[:, 0:2], rsum, None, ALU.mult))
                need(c_oh)
                mark(v.tensor_tensor(Mk[i], oh[i][:, 0, :], oh[i][:, 1, :], ALU.add))
                need(c_cw)
                link(v.tensor_scalar(weighted, oh[i][:, 0, :], rec[:, t, 0, 1:2], None, ALU.mult))
                v.scalar_tensor_tensor(stack[i][:, 0:64], oh[i][:, 1, :], rec[:, t, 1, 1:2], weighted,
                                       ALU.mult, ALU.add).then_inc(stack_ready, 1)

            def rank(t):
                i = t % 2
                dve.wait_ge(rank_ps, t + 1)
                v.tensor_copy(stackT[t], bank[7][0:97, 0:P]).then_inc(stackT_ready, 1)
                for k in range(2):
                    c_pos = mark(v.tensor_tensor_reduce(out=picked[:, k, :], in0=oh[i][:, k, :], in1=bank[7][:, 128:192],
                                                        scale=1.0, scalar=0.0, op0=ALU.mult, op1=ALU.add,
                                                        accum_out=pos[:, k:k + 1]))
                mark(v.tensor_tensor(C, C, Mk[i], ALU.add))
                need(c_pos)
                v.scalar_tensor_tensor(slot[:, t, :], idf[i], float(LIST), pos, ALU.mult, ALU.add).then_inc(rec_ready, 1)

            def add_shared(t):
                dve.wait_ge(z_ps, t + 1)
                v.tensor_tensor(X[:, t, :], X[:, t, :], z_bank[t][:, :], ALU.add).then_inc(z_added, 1)

            for s in range(1, NB + 2):
                if s <= NB:
                    relu_add(s - 1)
                if s >= 2:
                    route(s - 2)
                    if s == NB + 1:
                        for b in range(3):
                            add_shared(b)
                    rank(s - 2)
            link(v.tensor_scalar(caps, iota[0:1, 0:ROUNDS], float(CAP), None, ALU.mult))
            link(v.tensor_reduce(most, bank[7][0:1, 256:320], AX, ALU.max))
            link(v.tensor_scalar(over, caps, most, None, ALU.is_lt))
            link(v.tensor_reduce(nround, over, AX, ALU.add))
            v.tensor_copy(rounds_sb[0:1, 1:2], nround).then_inc(tokens_ready, 1)
            dve.wait_ge(tokens_ready, 1)
            R2 = dve.value_load(rounds_sb[0:1, 1:2], min_val=1, max_val=ROUNDS)
            with dve.Fori(0, R2) as r:
                dve.wait_ge(list_ps, r + 1)
                v.tensor_copy(TOK, bank[6][0:CAP, 0:64])
                v.tensor_scalar(DROW, bank[6][0:CAP, 0:64], spare[0:CAP, :], None, ALU.min)
                v.tensor_copy(CW, bank[6][0:CAP, 64:128]).then_inc(list_ready, 1)
                with dve.If(r < 1):
                    for b in range(3, 6):
                        add_shared(b)

                def rows(gi, u, count):
                    dve.wait_ge(xe_ps, count)
                    b = u % 2
                    for c in range(DC):
                        e = gi * RING + u
                        ins = v.tensor_scalar(xe[b][:, c, :], bank[b][:, c * CAP:(c + 1) * CAP], gT[:, c, ds(e, 1)],
                                              bT[:, c, ds(e, 1)], ALU.mult, ALU.add)
                    ins.then_inc(xe_ready, 1)

                rows(0, 0, r * EXPERTS + 1)
                with dve.If(r < 1):
                    for b in range(6, NB):
                        add_shared(b)

                def group(gi, last):
                    base = r * EXPERTS + gi * RING
                    for u in range(RING):
                        if not (last and u == RING - 1):
                            rows(gi, u + 1, base + u + 2)
                        dve.wait_ge(sl_ready, base + u + 1)
                        for m in range(HC):
                            ins = v.scalar_tensor_tensor(hT[u % 2][:, m, :], bank[4 + u % 2][:, m * CAP:(m + 1) * CAP],
                                                         b13T[:, 1, m, ds(gi * RING + u, 1)], sl[u % 2][:, m, :],
                                                         ALU.add, ALU.mult)
                        ins.then_inc(hT_ready, 1)

                with dve.Fori(0, GROUPS - 1) as gi:
                    group(gi, False)
                group(GROUPS - 1, True)
                for i in range(YS):
                    dve.wait_ge(y_out[i], (r + 1) * (16 * EXPERTS // YS))

        @block.tensor
        def _(pe):
            t = nc.tensor
            pe.wait_ge(consts, 5)
            pe.wait_ge(edge_prepped, 1)
            t.transpose(bank[0][:, 0:P], key, ident[:, :])
            t.transpose(bank[0][:, P:2 * P], slof, ident[:, :])
            t.transpose(bank[0][:, 2 * P:3 * P], edge_w, ident[:, :])
            t.matmul(bank[1][0:1, 0:P], mn, ident[:, :], start=True, stop=True)
            t.matmul(bank[1][0:1, P:2 * P], mx, ident[:, :], start=True, stop=True).then_inc(edges_transposed, 1)
            pe.wait_ge(base_ready, 1)
            t.matmul(bank[1][:, 384:512], ones[0:1, :], neg_base, start=True, stop=True).then_inc(base_ps, 1)
            pe.wait_ge(raw_in, 80)
            id64 = ident[0:64, 0:64]
            for i, raw in enumerate((raw_wg, raw_g, raw_b)):
                flat = raw.rearrange("e c d -> e (c d)")
                for c in range(DC):
                    ins = t.transpose(bank[2 + i // 2][:, (i % 2) * 256 + 64 * c:(i % 2) * 256 + 64 * c + 64],
                                      flat[:, c:c + DC * (P - 1) + 1:DC], id64)
                if i == 1:
                    ins.then_inc(raw_transposed, 1)
            for c in range(2 * HC):
                ins = t.transpose(bank[3][:, 256 + 64 * c:320 + 64 * c], raw_b13[:, c, :], id64)
            ins.then_inc(raw_transposed, 1)
            pe.wait_ge(edges_ready, 1)
            R1 = pe.value_load(rounds_sb[0:1, 0:1], min_val=1, max_val=N // WIN)

            def pair(r, j, with_x):
                half = pe.snap((r * (NB // 2) + j) * 4)
                quad = pe.snap(half * 2)
                for u in range(2):
                    if with_x:
                        pe.wait_ge(xh_ready, j * 2 + u + 1)
                        for c in range(DC):
                            ins = t.transpose(bank[4 + u][:, c * P:(c + 1) * P], xh[:, u, c:c + DC * (P - 1) + 1:DC], ident[:, :])
                        ins.then_inc(xhT_ps, 1)
                    for q in range(4 * u, 4 * u + 4):
                        if q % 2 == 0:
                            pe.wait_ge(osl_ready, half + (q // 2 + 1))
                        _, at = nc.values_load_multi_w_load_instructions(
                            tile_at[0:1, ds(j * 32 + QUAD * q, QUAD)], engines=[mybir.EngineType.PE],
                            min_val=0, max_val=QW - TW, skip_runtime_bounds_check_because="DVE bounded them by min, and a tile's window starts after its quad's")
                        pe.wait_ge(m_pool, quad + (q + 1))
                        pe.wait_ge(m_ready, quad + (q + 1))
                        pe.wait_ge(a_chain, quad + (q + 1))
                        if q == 2:
                            pe.wait_ge(raw_evac, 4)
                        t.matmul(bank[q % 4][:, 0:QW], ones[0:1, 0:P // 2].bitcast(bf16),
                                 zeros[0:1, :].unsqueeze(1).broadcast_to([1, QW // 64, 64]), start=True, stop=False)
                        for k in range(QUAD):
                            ins = t.matmul(bank[q % 4][:, ds(at[k], TW)], osl[:, (q // 2) % 2, (q % 2) * QUAD + k, :],
                                           Mq[q % 4][:, k, :], start=False, stop=(k == QUAD - 1))
                        ins.then_inc(quad_done[q % 2], 1)
                    if with_x:
                        pe.wait_ge(gw_in, 16)
                        pe.wait_ge(xhT_ready, j * 2 + u + 1)
                        for c in range(DC):
                            ins = t.matmul(bank[6 + u][:, :], xhT[:, u, c, :], GW[:, c, :], start=(c == 0), stop=(c == DC - 1))
                        ins.then_inc(hw_ps, 1)

            with pe.Fori(0, NB // 2) as j:
                pair(0, j, True)
            with pe.If(R1 > 1):
                with pe.Fori(1, R1) as r:
                    pe.wait_ge(win_chain, r * 6)
                    hold(pe)
                    with pe.Fori(0, NB // 2) as j:
                        pair(r, j, False)
            pe.wait_ge(a_chain, R1 * QUADS + 4)
            hold(pe)
            A3 = A[:, :].rearrange("p (n s) -> p n s", s=8)

            def transpose_a(s):
                for k in range(NB):
                    ins = t.transpose(bank[2 * (s % 2) + k // 4][:, (k % 4) * P:(k % 4 + 1) * P], A3[:, k * P:(k + 1) * P, s], ident[:, :])
                    if k % 4 == 3:
                        ins.then_inc(at_ps, 1)

            def sum_messages(s, ks):
                if ks[0] == 0:
                    pe.wait_ge(at_ready, 2 * s + 2)
                    if s >= 2:
                        pe.wait_ge(x1_ready, s - 1)
                for k in ks:
                    if s == 0 and k == NB - 1:
                        pe.wait_ge(hw_ready, NB)
                    ins = t.matmul(bank[4 + s % 2][:, :], AT[:, s % 2, k, :], HW[:, k, :], start=(k == 0), stop=(k == NB - 1))
                if ks[-1] == NB - 1:
                    ins.then_inc(out_ps, 1)

            def transpose_nx(b):
                pe.wait_ge(nx_ready, b + 1)
                if b >= 1:
                    pe.wait_ge(nxT_ready, b)
                for c in range(DC):
                    ins = t.transpose(bank[6][:, c * P:(c + 1) * P], nx[b % 2][:, c:c + DC * (P - 1) + 1:DC], ident[:, :])
                ins.then_inc(nxT_ps, 1)

            def route(b):
                pe.wait_ge(nxT_ready, b + 1)
                if b == 0:
                    pe.wait_ge(edges_ready, 3)
                elif b < NB - 1:
                    pe.wait_ge(rec_ready, b)
                for c in range(DC):
                    ins = t.matmul(route_bank[b][:, 0:P], nxT[b % 2][:, c, :], R[:, c, :], start=(c == 0), stop=(c == DC - 1))
                ins.then_inc(route_ps, 1)

            def rank(b):
                pe.wait_ge(stack_ready, b + 1)
                t.transpose(bank[7][0:97, 0:P], stack[b % 2], ident[:, :])
                t.matmul(bank[7][:, 128:192], before, Mk[b % 2], start=True, stop=False)
                if b >= 1:
                    pe.wait_ge(rec_ready, b)
                ins = t.matmul(bank[7][:, 128:192], ones[:, :], C, start=False, stop=True)
                if b == NB - 1:
                    t.matmul(bank[7][0:1, 256:320], ones[:, 0:1], Mk[b % 2], start=True, stop=False)
                    ins = t.matmul(bank[7][0:1, 256:320], ones[:, 0:1], C, start=False, stop=True)
                ins.then_inc(rank_ps, 1)

            def shared(b):
                pe.wait_ge(stackT_ready, b + 1)
                if b == 2:
                    pe.wait_ge(x1_ready, NB)
                if 3 <= b < 6:
                    pe.wait_ge(z_added, (1, 3, 2)[b - 3])
                if b == NB - 1:
                    pe.wait_ge(tokens_ready, 1)
                t.matmul(z_bank[b][:, :], stackT[b], stackB, start=True, stop=True).then_inc(z_ps, 1)

            transpose_a(0)
            pe.wait_ge(wsb_ready, 1)
            pe.wait_ge(hw_ready, NB)
            for c in range(DC):
                ins = t.matmul(bank[7][:, 0:64], ones[:, :], Wsb[:, c, :], start=(c == 0), stop=(c == DC - 1))
            ins.then_inc(sums_done, 1)
            for s in range(NB):
                if s + 1 < NB:
                    transpose_a(s + 1)
                if s >= 2:
                    sum_messages(s, range(0, 2))
                    route(s - 2)
                    sum_messages(s, range(2, 8))
                else:
                    sum_messages(s, range(0, 8))
                if s >= 1:
                    transpose_nx(s - 1)
                if s >= 2:
                    rank(s - 2)
            pe.wait_ge(at_ready, 2 * NB)
            route(NB - 2)
            for b in range(3):
                shared(b)
            transpose_nx(NB - 1)
            rank(NB - 2)
            route(NB - 1)
            rank(NB - 1)
            pe.wait_ge(tokens_ready, 1)
            R2 = pe.value_load(rounds_sb[0:1, 1:2], min_val=1, max_val=ROUNDS)
            with pe.Fori(0, R2) as r:
                pe.wait_ge(list_in, (r + 1) * 16)
                hold(pe)
                for a in range(2):
                    ins = t.transpose(bank[6][0:CAP, 64 * a:64 * a + 64], L[:, a:a + REC * (CAP - 1) + 1:REC], ident[0:64, 0:64])
                ins.then_inc(list_ps, 1)
                def rows(u, count):
                    pe.wait_ge(xg_in[u % XG], count * 16)
                    for c in range(DC):
                        ins = t.transpose(bank[u % 2][:, c * CAP:(c + 1) * CAP], xg[u % XG][:, c:c + DC * (P - 1) + 1:DC], ident[0:CAP, 0:CAP])
                    ins.then_inc(xe_ps, 1)

                with pe.If(r < 1):
                    for b in range(3, NB - 1):
                        shared(b)
                rows(0, r * GROUPS + 1)
                with pe.If(r < 1):
                    shared(NB - 1)

                def group(gi, last):
                    base = r * EXPERTS + gi * RING
                    turn = r * GROUPS + gi
                    uses = (r * GROUPS + gi + 1) * 48

                    def up(u):
                        if u < 2:
                            pe.wait_ge(z_added, (5, NB)[u])
                        pe.wait_ge(w_in[u], uses)
                        pe.wait_ge(xe_ready, base + u + 1)
                        for a, b in ((0, 2 + u % 2), (1, 4 + u % 2)):
                            for m in range(HC):
                                for c in range(DC):
                                    ins = t.matmul(bank[b][:, m * CAP:(m + 1) * CAP], w13[:, u, a, c, m * P:(m + 1) * P],
                                                   xe[u % 2][:, c, :], start=(c == 0), stop=(c == DC - 1))
                        ins.then_inc(h_ps, 1)

                    def down(u):
                        pe.wait_ge(hT_ready, base + u + 1)
                        for m in range(HC):
                            ins = t.matmul(bank[6 + u % 2][0:CAP, :], hT[u % 2][:, m, :], w2[:, u, m, :],
                                           start=(m == 0), stop=(m == HC - 1))
                        ins.then_inc(y_ps, 1)

                    for u in range(RING):
                        if not (last and u == RING - 1):
                            rows(u + 1, turn + ((u + 1) // XG + 1))
                        up(u)
                        if u:
                            down(u - 1)
                    down(RING - 1)

                with pe.Fori(0, GROUPS - 1) as gi:
                    group(gi, False)
                group(GROUPS - 1, True)
                pe.wait_ge(y_ready, (r + 1) * EXPERTS)


_INS = ['x', 'src', 'dst', 'edge_weight', 'L0_gnn_W', 'L0_gnn_bias', 'L0_ffn_Wg', 'L0_ffn_bg', 'L0_ffn_gamma',
        'L0_ffn_beta', 'L0_ffn_W1', 'L0_ffn_b1', 'L0_ffn_W3', 'L0_ffn_b3', 'L0_ffn_W2', 'L0_ffn_b2', 'L0_ffn_gs',
        'L0_ffn_bs', 'L0_ffn_Ws1', 'L0_ffn_bs1', 'L0_ffn_Ws3', 'L0_ffn_bs3', 'L0_ffn_Ws2', 'L0_ffn_bs2']


def kernel(**inputs):
    import numpy as _np
    import concourse.bacc as _bacc
    from concourse import mybir as _mybir
    from concourse.bass_utils import run_bass_kernel_spmd as _run

    nc = _bacc.Bacc("TRN2", target_bir_lowering=False, num_devices=1)
    arrays, args = {}, []
    for name in _INS:
        a = _np.ascontiguousarray(inputs[name])
        arrays[f"in_{name}_dram"] = a
        args.append(nc.dram_tensor(f"in_{name}_dram", a.shape, _mybir.dt.from_np(a.dtype), kind="ExternalInput").ap())
    out = nc.dram_tensor("out_dram", (N, D), _mybir.dt.float32, kind="ExternalOutput").ap()
    moe_gnn(nc, *args, out)
    r = _run(nc, [arrays], core_ids=[0])
    return r.results[0]["out_dram"]
```
